# Optimizing a Trainium2 kernel written in Bass

```python
import numpy as np
import jax
import jax.numpy as jnp

def _softmax(x, axis=-1):
    return jax.nn.softmax(x, axis=axis)
def _gelu(x):
    return jax.nn.gelu(x, approximate=True)
def _silu(x):
    return jax.nn.silu(x)
def _sigmoid(x):
    return jax.nn.sigmoid(x)
def _layernorm(x, axis=-1, eps=1e-5):
    m = jnp.mean(x, axis=axis, keepdims=True)
    v = jnp.var(x, axis=axis, keepdims=True)
    return (x - m) / jnp.sqrt(v + eps)
def _scatter_add(tgt, idx, src, axis=0):
    return tgt.at[idx].add(src)
def _segment_sum(src, seg, n):
    return jax.ops.segment_sum(src, seg, n)

kernel_name = 'mk_conv_preact_d2_conv_nhwc128_a2073f'

def setup_inputs(seed: int = 0):
    np.random.seed(seed)
    _w = jnp.asarray
    def _rec_inputs():
        import jax
        import jax.numpy as jnp
        _gk = jax.random.key(seed)
        x = -0.000125 + 0.9999 * jax.random.normal(jax.random.fold_in(_gk, 1), (16, 128, 128, 128), jnp.float32)
        return x
    x = _rec_inputs()
    def _L0_conv_setup():
        import jax, jax.numpy as jnp
        import numpy as np
        B, H, W, C, K, T = (16, 128, 128, 64, 7, 16)
        C2 = 2 * C

        def _pad_and_fft(kr, ki, h, w, k):
            kern = kr + 1j * ki
            ph = (h - k) // 2
            pw = (w - k) // 2
            padded = jnp.pad(kern, ((0, 0), (ph, h - k - ph), (pw, w - k - pw)))
            return jnp.fft.fft2(padded, axes=(-2, -1))
        key = jax.random.key(seed)
        ks = jax.random.split(key, 12)
        d = {'x_ri': jax.random.normal(ks[0], (B, H, W, C2), jnp.float32), 'Wf': jax.random.normal(ks[1], (C2, C2), jnp.float32) * 0.05, 'bf': jnp.zeros((C2,), jnp.float32), 'Wi': jax.random.normal(ks[2], (C2, C2), jnp.float32) * 0.05, 'bi': jnp.zeros((C2,), jnp.float32), 'Wd': jax.random.normal(ks[3], (C2, C2), jnp.float32) * 0.05, 'bd': jnp.zeros((C2,), jnp.float32), 'A_real': jax.random.normal(ks[4], (C, K, K), jnp.float32) * 0.02, 'A_imag': jax.random.normal(ks[5], (C, K, K), jnp.float32) * 0.02, 'B_real': jax.random.normal(ks[6], (C, K, K), jnp.float32) * 0.02, 'B_imag': jax.random.normal(ks[7], (C, K, K), jnp.float32) * 0.02}
        return d
    _L0_conv_all = _L0_conv_setup()
    _L0_conv_in = {k: v for k, v in _L0_conv_all.items() if k in ('Wf', 'bf', 'Wi', 'bi', 'Wd', 'bd', 'A_real', 'A_imag', 'B_real', 'B_imag', )}
    del _L0_conv_all

    def _L1_conv_setup():
        import jax, jax.numpy as jnp
        import numpy as np
        EPS = 1e-06

        def kernel_to_freq_2d(kernel, H, W):
            C, kh, kw = kernel.shape
            th = (jnp.arange(kh) - kh // 2) % H
            tw = (jnp.arange(kw) - kw // 2) % W
            TH, TW = jnp.meshgrid(th, tw, indexing='ij')
            padded = jnp.zeros((C, H, W), dtype=kernel.dtype).at[:, TH, TW].set(kernel)
            return jnp.fft.fft2(padded, axes=(1, 2))

        def heinsen_scan_log(log_coeffs, log_values):

            def op(left, right):
                la, lb = left
                ra, rb = right
                return (la + ra, jnp.logaddexp(ra + lb, rb))
            _, log_h = jax.lax.associative_scan(op, (log_coeffs, log_values), axis=0)
            return log_h
        key = jax.random.key(seed)
        ks = jax.random.split(key, 7)
        B, H, W, C, k = (4, 128, 128, 128, 7)
        fan_in = k * k
        x = jax.random.normal(ks[0], (B, H, W, C), dtype=jnp.float32)
        A_kernel = jax.random.normal(ks[1], (C, k, k), dtype=jnp.float32) / np.sqrt(fan_in)
        B_kernel = jax.random.normal(ks[2], (C, k, k), dtype=jnp.float32) / np.sqrt(fan_in)
        gate_A_kernel = jax.random.normal(ks[3], (C, k, k), dtype=jnp.float32) * 0.02
        gate_B_kernel = jax.random.normal(ks[4], (C, k, k), dtype=jnp.float32) * 0.02
        W_out = jax.random.normal(ks[5], (C, C), dtype=jnp.float32) / np.sqrt(C)
        b_out = jnp.zeros((C,), dtype=jnp.float32)
        return dict(x=x, A_kernel=A_kernel, B_kernel=B_kernel, gate_A_kernel=gate_A_kernel, gate_B_kernel=gate_B_kernel, W_out=W_out, b_out=b_out, T=8)
    _L1_conv_all = _L1_conv_setup()
    _L1_conv_in = {k: v for k, v in _L1_conv_all.items() if k in ('A_kernel', 'B_kernel', 'gate_A_kernel', 'gate_B_kernel', 'W_out', 'b_out', )}
    del _L1_conv_all

    return {
        "x": x,
        "L0_conv_Wf": _L0_conv_in["Wf"],
        "L0_conv_bf": _L0_conv_in["bf"],
        "L0_conv_Wi": _L0_conv_in["Wi"],
        "L0_conv_bi": _L0_conv_in["bi"],
        "L0_conv_Wd": _L0_conv_in["Wd"],
        "L0_conv_bd": _L0_conv_in["bd"],
        "L0_conv_A_real": _L0_conv_in["A_real"],
        "L0_conv_A_imag": _L0_conv_in["A_imag"],
        "L0_conv_B_real": _L0_conv_in["B_real"],
        "L0_conv_B_imag": _L0_conv_in["B_imag"],
        "L1_conv_A_kernel": _L1_conv_in["A_kernel"],
        "L1_conv_B_kernel": _L1_conv_in["B_kernel"],
        "L1_conv_gate_A_kernel": _L1_conv_in["gate_A_kernel"],
        "L1_conv_gate_B_kernel": _L1_conv_in["gate_B_kernel"],
        "L1_conv_W_out": _L1_conv_in["W_out"],
        "L1_conv_b_out": _L1_conv_in["b_out"],
    }

def reference(x, L0_conv_Wf, L0_conv_bf, L0_conv_Wi, L0_conv_bi, L0_conv_Wd, L0_conv_bd, L0_conv_A_real, L0_conv_A_imag, L0_conv_B_real, L0_conv_B_imag, L1_conv_A_kernel, L1_conv_B_kernel, L1_conv_gate_A_kernel, L1_conv_gate_B_kernel, L1_conv_W_out, L1_conv_b_out):
    import jax
    import jax.numpy as jnp
    def _L0_conv_ref(x_ri, Wf, bf, Wi, bi, Wd, bd, A_real, A_imag, B_real, B_imag):
        import jax, jax.numpy as jnp
        import numpy as np
        B, H, W, C, K, T = (16, 128, 128, 64, 7, 16)
        C2 = 2 * C

        def _pad_and_fft(kr, ki, h, w, k):
            kern = kr + 1j * ki
            ph = (h - k) // 2
            pw = (w - k) // 2
            padded = jnp.pad(kern, ((0, 0), (ph, h - k - ph), (pw, w - k - pw)))
            return jnp.fft.fft2(padded, axes=(-2, -1))
        b, h, w, c2 = x_ri.shape
        c = c2 // 2
        k = A_real.shape[-1]
        forget_gate = jax.nn.sigmoid(x_ri @ Wf + bf + 2.0)
        input_gate = jax.nn.sigmoid(x_ri @ Wi + bi)
        delta = jax.nn.softplus(x_ri @ Wd + bd) * 0.1
        A_f = _pad_and_fft(A_real, A_imag, h, w, k)
        B_f = _pad_and_fft(B_real, B_imag, h, w, k)
        A_ri = jnp.concatenate([A_f.real, A_f.imag], 0).transpose(1, 2, 0)[None]
        B_ri = jnp.concatenate([B_f.real, B_f.imag], 0).transpose(1, 2, 0)[None]
        Ar, Ai = (A_ri[..., :c], A_ri[..., c:])
        mag = jnp.sqrt(Ar ** 2 + Ai ** 2 + 1e-08)
        scale = 0.95 * jax.nn.sigmoid(mag) / (mag + 1e-08)
        Ar = Ar * scale
        Ai = Ai * scale
        Br, Bi_ = (B_ri[..., :c], B_ri[..., c:])
        x_r, x_i = (x_ri[..., :c], x_ri[..., c:])
        Bx_r = Br * x_r - Bi_ * x_i
        Bx_i = Br * x_i + Bi_ * x_r
        inp_r = delta[..., :c] * input_gate[..., :c] * Bx_r
        inp_i = delta[..., c:] * input_gate[..., c:] * Bx_i
        fg_r, fg_i = (forget_gate[..., :c], forget_gate[..., c:])

        def step(h_state, _):
            h_r, h_i = h_state
            Ah_r = Ar * h_r - Ai * h_i
            Ah_i = Ar * h_i + Ai * h_r
            return ((fg_r * Ah_r + inp_r, fg_i * Ah_i + inp_i), None)
        h0 = (jnp.zeros_like(x_r), jnp.zeros_like(x_i))
        (h_r, h_i), _ = jax.lax.scan(step, h0, None, length=T)
        return jnp.concatenate([h_r, h_i], axis=-1)

    def _L1_conv_ref(x, A_kernel, B_kernel, gate_A_kernel, gate_B_kernel, W_out, b_out, T):
        import jax, jax.numpy as jnp
        import numpy as np
        EPS = 1e-06

        def kernel_to_freq_2d(kernel, H, W):
            C, kh, kw = kernel.shape
            th = (jnp.arange(kh) - kh // 2) % H
            tw = (jnp.arange(kw) - kw // 2) % W
            TH, TW = jnp.meshgrid(th, tw, indexing='ij')
            padded = jnp.zeros((C, H, W), dtype=kernel.dtype).at[:, TH, TW].set(kernel)
            return jnp.fft.fft2(padded, axes=(1, 2))

        def heinsen_scan_log(log_coeffs, log_values):

            def op(left, right):
                la, lb = left
                ra, rb = right
                return (la + ra, jnp.logaddexp(ra + lb, rb))
            _, log_h = jax.lax.associative_scan(op, (log_coeffs, log_values), axis=0)
            return log_h
        B, H, W, C = x.shape

        def ifft_real(z_bhwc):
            return jnp.fft.ifft2(z_bhwc.transpose(0, 3, 1, 2), axes=(2, 3)).real.transpose(0, 2, 3, 1)
        A_f = kernel_to_freq_2d(A_kernel, H, W).transpose(1, 2, 0)
        B_f = kernel_to_freq_2d(B_kernel, H, W).transpose(1, 2, 0)
        gA_f = kernel_to_freq_2d(gate_A_kernel, H, W).transpose(1, 2, 0)
        gB_f = kernel_to_freq_2d(gate_B_kernel, H, W).transpose(1, 2, 0)
        x_f = jnp.fft.fft2(x.transpose(0, 3, 1, 2), axes=(2, 3)).transpose(0, 2, 3, 1)
        gate_A = jax.nn.sigmoid(ifft_real(gA_f[None] * x_f))
        gate_B = jax.nn.sigmoid(ifft_real(gB_f[None] * x_f))
        a_spatial = ifft_real(jnp.broadcast_to(A_f[None], (B, H, W, C)))
        b_spatial = ifft_real(B_f[None] * x_f)
        a_t = a_spatial * gate_A
        b_t = b_spatial * gate_B
        gate_seq = jnp.tile(a_t[None], (T, 1, 1, 1, 1))
        h_tilde_seq = jnp.tile(b_t[None], (T, 1, 1, 1, 1))
        log_z = -jax.nn.softplus(-gate_seq)
        log_coeffs = -jax.nn.softplus(gate_seq)
        log_values = log_z + jnp.log(jax.nn.softplus(h_tilde_seq) + EPS)
        log_h = heinsen_scan_log(log_coeffs, log_values)
        h_final = jnp.exp(log_h[-1])
        return h_final @ W_out + b_out

    def _gn(v, G=32, eps=1e-5):
        B_, H_, W_, C_ = v.shape
        g = v.reshape(B_, H_, W_, G, C_ // G)
        m = jnp.mean(g, axis=(1, 2, 4), keepdims=True)
        s = jnp.var(g, axis=(1, 2, 4), keepdims=True)
        return ((g - m) / jnp.sqrt(s + eps)).reshape(v.shape)

    def _ln_c(v, eps=1e-6):
        m = jnp.mean(v, axis=-1, keepdims=True)
        s = jnp.var(v, axis=-1, keepdims=True)
        return (v - m) / jnp.sqrt(s + eps)

    def _ln_t(v, eps=1e-5):
        m = jnp.mean(v, axis=-1, keepdims=True)
        s = jnp.var(v, axis=-1, keepdims=True)
        return (v - m) / jnp.sqrt(s + eps)

    def _to_tokens(v):
        B_, H_, W_, C_ = v.shape
        return v.reshape(B_, H_ * W_, C_)
    def _from_tokens(t, like):
        return t.reshape(like.shape)

    x = x + _L0_conv_ref(_gn(x), L0_conv_Wf, L0_conv_bf, L0_conv_Wi, L0_conv_bi, L0_conv_Wd, L0_conv_bd, L0_conv_A_real, L0_conv_A_imag, L0_conv_B_real, L0_conv_B_imag)
    x = x + _L1_conv_ref(_gn(x), L1_conv_A_kernel, L1_conv_B_kernel, L1_conv_gate_A_kernel, L1_conv_gate_B_kernel, L1_conv_W_out, L1_conv_b_out, 8)
    return x


_drawn_inputs = setup_inputs


def setup_inputs(seed=0):
    import zlib

    import numpy as np

    out = dict(_drawn_inputs(seed))
    spreads = {'L0_conv_bf': (0.0, 0.8),
     'L0_conv_bi': (0.0, 0.8),
     'L0_conv_bd': (0.0, 0.8),
     'L1_conv_b_out': (0.0, 0.1)}
    factors = {'L0_conv_Wf': 8.0,
     'L0_conv_Wi': 8.0,
     'L0_conv_Wd': 8.0,
     'L0_conv_A_real': 8.0,
     'L0_conv_A_imag': 8.0,
     'L0_conv_B_real': 8.0,
     'L0_conv_B_imag': 8.0,
     'L1_conv_A_kernel': 8.0,
     'L1_conv_gate_A_kernel': 8.0,
     'L1_conv_gate_B_kernel': 3.761}
    for name, (base, spread) in spreads.items():
        noise = np.random.default_rng([zlib.crc32(name.encode()), seed]).standard_normal(out[name].shape)
        drawn = base * np.exp(spread * noise) if base else spread * noise
        out[name] = jnp.asarray(drawn.astype(out[name].dtype))
    for name, factor in factors.items():
        out[name] = (out[name] * factor).astype(out[name].dtype)
    return out
```

```python
from contextlib import ExitStack

import numpy as np
import concourse.bass as bass
from concourse import mybir

F32 = mybir.dt.float32
F32R = mybir.dt.float32r
BF16 = mybir.dt.bfloat16
ALU = mybir.AluOpType
ACT = mybir.ActivationFunctionType
AX = mybir.AxisListType

P = 128
B, H, W, C = 16, 128, 128, 128
CH = C // 2
TAPS = 7
G = 32
CG = C // G
WB = 32
NWB = W // WB
TILES = NWB * B
SW = 8
SUBS = WB // SW
HALF = SW * CH
FULL = SW * C
GN_EPS = 1e-5
TINY = 2.0 ** -63


def view(ap, *dims):
    return bass.AP(ap.tensor, ap.offset, [list(ap.ap[0])] + [list(d) for d in dims])


def stats_of_x(nc, x, rstd_c, nmr_c, ones_n, mask):
    NPX = B * G
    with ExitStack() as ctx:
        img = [ctx.enter_context(nc.sbuf_tensor(f"img{i}", [P, W * C], F32)) for i in range(2)]
        st = ctx.enter_context(nc.sbuf_tensor("xst", [P, B, G, 6], F32))
        dev = ctx.enter_context(nc.sbuf_tensor("xdev", [P, 2, NPX], F32))
        m2 = ctx.enter_context(nc.sbuf_tensor("xm2", [P, NPX], F32))
        mean = ctx.enter_context(nc.sbuf_tensor("xmean", [P, NPX], F32))
        sd = ctx.enter_context(nc.sbuf_tensor("xsd", [P, NPX], F32))
        rs = ctx.enter_context(nc.sbuf_tensor("xrs", [P, NPX], F32))
        mps = ctx.enter_context(nc.psum_tensor("xmean_ps", [P, NPX], F32))
        vps = ctx.enter_context(nc.psum_tensor("xvar_ps", [P, NPX], F32))
        img_in = [ctx.enter_context(nc.semaphore(f"img_in{i}")) for i in range(2)]
        counted = ctx.enter_context(nc.semaphore("counted"))
        mean_ready = ctx.enter_context(nc.semaphore("mean_ready"))
        var_ready = ctx.enter_context(nc.semaphore("var_ready"))
        sd_ready = ctx.enter_context(nc.semaphore("sd_ready"))
        steps = ctx.enter_context(nc.semaphore("xsteps"))
        block = ctx.enter_context(nc.Block())

        @block.sync
        def _(sp):
            for u in range(2):
                sp.dma_start(img[u][:, :], x[u].rearrange("h w c -> h (w c)")).then_inc(img_in[u], 16)
            with sp.Fori(0, B // 2 - 1) as i:
                for u in range(2):
                    sp.wait_ge(counted, (i * 2 + (u + 1)) * G)
                    src = x[bass.ds(i * 2 + (2 + u), 1)].rearrange("a h w c -> (a h) (w c)")
                    sp.dma_start(img[u][:, :], src).then_inc(img_in[u], 16)

        @block.vector
        def _(v):
            with v.Fori(0, B // 2) as i:
                for u in range(2):
                    v.wait_ge(img_in[u], (i + 1) * 16)
                    for g in range(G):
                        v.bn_stats(st[:, bass.ds(i * 2 + u, 1), g, :],
                                   view(img[u][:, g * CG:g * CG + 1], [C, W], [1, CG])).then_inc(counted, 1)
            n = [0]

            def step(ins):
                ins.then_inc(steps, 1)
                n[0] += 1
                v.wait_ge(steps, n[0])

            fl = st[:, :, :, :].rearrange("p b g s -> p (b g) s")
            v.wait_ge(mean_ready, 1)
            step(v.tensor_tensor(dev[:, 0, :], fl[:, :, 1], mps[:, :], ALU.subtract))
            step(v.tensor_tensor(dev[:, 1, :], fl[:, :, 4], mps[:, :], ALU.subtract))
            step(v.tensor_copy(mean[:, :], mps[:, :]))
            step(v.tensor_tensor(m2[:, :], fl[:, :, 2], fl[:, :, 5], ALU.add))
            step(v.tensor_tensor(dev[:, :, :], dev[:, :, :], dev[:, :, :], ALU.mult))
            step(v.tensor_tensor(dev[:, 0, :], dev[:, 0, :], dev[:, 1, :], ALU.add))
            step(v.scalar_tensor_tensor(dev[:, 0, :], m2[:, :], 1.0 / (W * CG // 2), dev[:, 0, :],
                                        ALU.mult, ALU.add))
            v.wait_ge(var_ready, 1)
            step(v.tensor_scalar(m2[:, :], vps[:, :], GN_EPS, None, ALU.add))
            v.wait_ge(sd_ready, 1)
            step(v.reciprocal(rs[:, :], sd[:, :]))
            step(v.scalar_tensor_tensor(mean[:, :], mean[:, :], -1.0, rs[:, :], ALU.mult, ALU.mult))
            for src, dst in ((rs, rstd_c), (mean, nmr_c)):
                step(v.tensor_tensor(dev[:, 0, :].rearrange("p (b g) -> p b g", g=G),
                                     src[:, :].rearrange("p (b g) -> p b g", g=G),
                                     view(mask[:, 0:1], [0, B], [1, G]), ALU.mult))
                step(v.reduce_sum(dst[:, :], dev[:, 0, :].rearrange("p (b g) -> p b g", g=G), axis=AX.X))

        @block.tensor
        def _(pe):
            fl = st[:, :, :, :].rearrange("p b g s -> p (b g) s")
            pe.wait_ge(counted, B * G)
            pe.matmul(mps[:, :], ones_n[:, :], fl[:, :, 1], start=True, stop=False)
            pe.matmul(mps[:, :], ones_n[:, :], fl[:, :, 4], start=False, stop=True).then_inc(mean_ready, 1)
            pe.wait_ge(steps, 7)
            pe.matmul(vps[:, :], ones_n[:, :], dev[:, 0, :], start=True, stop=True).then_inc(var_ready, 1)

        @block.scalar
        def _(act):
            act.wait_ge(steps, 8)
            act.activation(sd[:, :], m2[:, :], ACT.Sqrt).then_inc(sd_ready, 1)


def setup(nc, d, s, rows_dram):
    with ExitStack() as ctx:
        raw = ctx.enter_context(nc.sbuf_tensor("bias_raw", [1, 4, C], F32))
        rest = ctx.enter_context(nc.sbuf_tensor("bias_rest", [1, 4, C], F32))
        parts = ctx.enter_context(nc.sbuf_tensor("bias_parts", [1, 3, 4, C], BF16))
        kmraw = ctx.enter_context(nc.sbuf_tensor("km_raw", [2 * TAPS * TAPS, 4 * CH], F32))
        kmsign = ctx.enter_context(nc.sbuf_tensor("km_sign", [2 * TAPS * TAPS, 4 * CH], F32))
        taps = ctx.enter_context(nc.sbuf_tensor("taps", [C, 3 * TAPS, TAPS], F32))
        rows = ctx.enter_context(nc.sbuf_tensor("rows", [C, 3 * TAPS, 256], F32))
        loaded = ctx.enter_context(nc.semaphore("consts_in"))
        steps = ctx.enter_context(nc.semaphore("setup_steps"))
        placed = ctx.enter_context(nc.semaphore("parts_placed"))
        rows_out = ctx.enter_context(nc.semaphore("rows_out"))
        block = ctx.enter_context(nc.Block())

        @block.sync
        def _(sp):
            n = 0
            for dst, src in ((taps[:, :, :], d["taps"]), (raw[:, 0, :], d["bf"]), (raw[:, 1, :], d["bi"]),
                             (raw[:, 2, :], d["bd"]), (raw[:, 3, :], d["b_out"]),
                             (kmraw[:, :], d["km"]), (kmsign[:, :], d["km_sign"]),
                             (s["wfi"][:, 0:C], d["Wf"]), (s["wfi"][:, C:2 * C], d["Wi"]), (s["wd"][:, :], d["Wd"]),
                             (s["wout"][:, :], d["W_out"]), (s["ident"][:, :], d["ident"]),
                             (s["mask"][:, :], d["mask"]), (s["apad"][:, :, :], d["apad"])):
                sp.dma_start(dst, src).then_inc(loaded, 16)
                n += 16
            assert n == 14 * 16
            sp.wait_ge(steps, 14)
            for k in range(3):
                for r in range(2):
                    sp.dma_start(s["b_fi"][k:k + 1, r, :], parts[:, k, 0:2, :].rearrange("p a c -> p (a c)")).then_inc(placed, 16)
                for r in range(4):
                    sp.dma_start(s["b_d"][k:k + 1, r, :], parts[:, k, 2, :]).then_inc(placed, 16)
                    sp.dma_start(s["b_o"][k:k + 1, r, :], parts[:, k, 3, :]).then_inc(placed, 16)
            sp.dma_start(rows_dram, rows[:, :, :].rearrange("c q n -> c (q n)")).then_inc(rows_out, 16)
            sp.wait_ge(placed, 3 * 10 * 16)
            sp.wait_ge(rows_out, 16)

        @block.vector
        def _(v):
            n = [0]

            def step(ins):
                ins.then_inc(steps, 1)
                n[0] += 1
                v.wait_ge(steps, n[0])

            step(v.memset(s["ones_n"][:, :], 1.0 / (2 * P)))
            step(v.memset(s["ones3"][:, :], 1.0))
            step(v.memset(s["tiny"][:, :], TINY))
            step(v.memset(rows[:, :, :], 0.0))
            v.wait_ge(loaded, 14 * 16)
            step(v.tensor_copy(rows[:, :, 124:131], taps[:, :, :]))
            step(v.tensor_copy(rows[:, :, 0:3], taps[:, :, 4:7]))
            step(v.tensor_copy(rows[:, :, 252:255], taps[:, :, 0:3]))
            step(v.tensor_scalar(raw[:, 0, :], raw[:, 0, :], 2.0, None, ALU.add))
            step(v.tensor_copy(parts[:, 0, :, :], raw[:, :, :]))
            step(v.tensor_tensor(rest[:, :, :], raw[:, :, :], parts[:, 0, :, :], ALU.subtract))
            step(v.tensor_copy(parts[:, 1, :, :], rest[:, :, :]))
            step(v.tensor_tensor(raw[:, :, :], rest[:, :, :], parts[:, 1, :, :], ALU.subtract))
            step(v.tensor_copy(parts[:, 2, :, :], raw[:, :, :]))
            step(v.tensor_tensor(s["km"][:, :], kmraw[:, :], kmsign[:, :], ALU.mult))


V_STEPS = ("m1 m2 fs p t d sp bxr bxi t2 g b1 v a1 t4 b2 s0 ep q0 s q er g1 y negx nry rx sy snx syd syt u "
           "alpha beta w av n1 n2 ax mr mi fm out").split()
V = {n: i + 1 for i, n in enumerate(V_STEPS)}
KV = len(V_STEPS)
A_STEPS = "ev0 ev1 fi0 fi1 sd ln tt d2 t2t2 d4 t4t4".split()
A = {n: i + 1 for i, n in enumerate(A_STEPS)}
KA = len(A_STEPS)


def layer0(nc, x, x1, basis, s):
    with ExitStack() as ctx:
        def sb(name, shape, dt=F32):
            return ctx.enter_context(nc.sbuf_tensor(name, shape, dt))

        def sem(name):
            return ctx.enter_context(nc.semaphore(name))

        xt = [sb(f"xt{i}", [P, WB, C]) for i in range(2)]
        ot = [sb(f"ot{i}", [P, C, WB]) for i in range(2)]
        tab = {n: sb(f"tab_{n}", [P, WB * CH]) for n in ("Ar", "Ai", "A2", "Br", "Bi")}
        xnT = [sb(f"xnT{i}", [P, SW, P]) for i in range(2)]
        fi = [sb(f"fi{i}", [P, SW, 2 * C]) for i in range(2)]
        ld = [sb(f"ld{i}", [P, FULL]) for i in range(2)]
        NT = 20
        tmp = sb("tmp", [P, NT, HALF])
        ebuf = tmp[0:2 * TAPS * TAPS, 12:20, :].rearrange("p a n -> p (a n)").rearrange("p (w h) -> p w h", h=P)
        m1, m2, bx, sp_, av = (sb(n, [P, FULL]) for n in ("m1", "m2", "bx", "spg", "av"))
        pT = ctx.enter_context(nc.psum_tensor("pT", [P, 2, 512], F32))
        pZ = ctx.enter_context(nc.psum_tensor("pZ", [P, 4, 512], F32))
        pD = ctx.enter_context(nc.psum_tensor("pD", [P, 2, 512], F32))
        x_in, x1_out = [sem(f"x_in{i}") for i in range(2)], [sem(f"x1_out{i}") for i in range(2)]
        e_in = sem("e_in")
        pe_xT, pe_z, pe_xn = sem("pe_xT"), sem("pe_z"), sem("pe_xn")
        v_done, a_done = sem("v_done"), sem("a_done")
        scale, shift = ([sb(f"{n}{i}", [C, 1]) for i in range(2)] for n in ("scale", "shift"))
        scale_set = sem("scale_set")
        tab_pe, tab_v, tab_a = sem("tab_pe"), sem("tab_v"), sem("tab_a")
        block = ctx.enter_context(nc.Block())

        (t, d, tt, d2, t2, t2t2, t4, d4, t4t4, b1, a1, ss, q, er, ep, g1, y, negx, nry, rx) = (
            tmp[:, i, :] for i in range(NT))

        def vn(sblk, name, back=0):
            return sblk * KV + ((2 - back) * KV + V[name])

        def an(sblk, name, back=0):
            return sblk * KA + ((2 - back) * KA + A[name])

        def xTn(sblk, j):
            return sblk * 2 + (j + 1)

        def zn(sblk, j):
            return sblk * 3 + (j + 1)

        def xnn(sblk, j, back=0):
            return sblk * 2 + (4 - 2 * back + j + 1)

        TV = 27
        TA = 2

        def blocks(eng, tables, body):
            with eng.Fori(0, NWB) as wb:
                tables(wb)
                with eng.Fori(0, B // 2) as ip:
                    for u in range(2):
                        tile = wb * B + ip * 2 + u
                        for k in range(SUBS):
                            body(wb, ip * 2 + u, wb * (B // 2) + ip, tile * SUBS + k, u, k)

        @block.sync
        def _(sp):
            for u in range(2):
                sp.sem_inc(x1_out[u], 16)
            with sp.Fori(0, NWB) as wb:
                def load(b, u):
                    sp.dma_start(xt[u][:, :, :].rearrange("p w c -> p (w c)"),
                                 x[bass.ds(b, 1), :, bass.ds(wb * WB, WB), :].rearrange("a h w c -> (a h) (w c)")
                                 ).then_inc(x_in[u], 16)

                def store(b, u):
                    sp.wait_ge(v_done, vn((wb * B + b) * SUBS + 3, "out"))
                    dst = x1[:, :, bass.ds(b, 1), bass.ds(wb, 1), :, :].rearrange("g h a e c w -> h g (a e c w)")
                    sp.dma_start(dst, ot[u][:, :, :].rearrange("p (g c) w -> p g (c w)", g=G)).then_inc(x1_out[u], 16)

                sp.wait_ge(tab_pe, wb * 4 + 1)
                sp.dma_start(ebuf, basis[:, bass.ds(wb * WB, WB), :]).then_inc(e_in, 16)
                for u in range(2):
                    load(u, u)
                with sp.Fori(0, B // 2 - 1) as ip:
                    for u in range(2):
                        store(ip * 2 + u, u)
                        load(ip * 2 + (2 + u), u)
                for u in range(2):
                    store(B - 2 + u, u)
            for u in range(2):
                sp.wait_ge(x1_out[u], 16 * (TILES // 2 + 1))

        @block.tensor
        def _(pe):
            pe.sem_inc(pe_xn, 4)
            pe.sem_inc(tab_pe, 1)

            def tables(wb):
                pe.wait_ge(e_in, (wb + 1) * 16)
                pe.wait_ge(a_done, an(wb * (B * SUBS), "fi1", back=1))
                for j in range(4):
                    pe.wait_ge(tab_v, wb * TV + (4 * j + 1))
                    for w in range(SW):
                        last = pe.matmul(pZ[:, w // 2, (w % 2) * 256:(w % 2) * 256 + 256],
                                         ebuf[:, j * SW + w, :], s["km"][:, :], start=True, stop=True)
                    last.then_inc(tab_pe, 1)

            def body(wb, b, pair, sblk, u, k):
                par = k % 2
                if k == 0:
                    pe.wait_ge(x_in[u], (pair + 1) * 16)
                for j in range(2):
                    pe.wait_ge(v_done, vn(sblk, "m2", back=1))
                    for w in range(4):
                        last = pe.transpose(pT[:, j, w * P:(w + 1) * P], xt[u][:, k * SW + 4 * j + w, :], s["ident"][:, :])
                    last.then_inc(pe_xT, 1)
                for j in range(2):
                    pe.wait_ge(a_done, an(sblk, f"ev{j}"))
                    for bank in (2 * j, 2 * j + 1):
                        pe.matmul(pZ[:, bank, :], s["ones3"][0:3, :], s["b_fi"][0:3, :, :], start=True, stop=False)
                        for w in (2 * bank, 2 * bank + 1):
                            last = pe.matmul(pZ[:, bank, (w % 2) * 256:(w % 2) * 256 + 256], xnT[par][:, w, :],
                                             s["wfi"][:, :], start=False, stop=w % 2 == 1)
                    last.then_inc(pe_z, 1)
                pe.wait_ge(v_done, vn(sblk, "sp", back=1))
                for bank in range(2):
                    pe.matmul(pD[:, bank, :], s["ones3"][0:3, :], s["b_d"][0:3, :, :], start=True, stop=False)
                    for w in range(4):
                        last = pe.matmul(pD[:, bank, w * C:(w + 1) * C], xnT[par][:, 4 * bank + w, :],
                                         s["wd"][:, :], start=False, stop=w == 3)
                last.then_inc(pe_z, 1)
                for j in range(2):
                    for w in range(4):
                        last = pe.transpose(pT[:, j, w * P:(w + 1) * P], xnT[par][:, 4 * j + w, :], s["ident"][:, :])
                    last.then_inc(pe_xn, 1)

            blocks(pe, tables, body)

        @block.scalar
        def _(act):
            act.sem_inc(a_done, 2 * KA)

            def tables(wb):
                act.wait_ge(tab_v, wb * TV + (1 + 19))
                mag = tmp[:, 0:4, :].rearrange("p a n -> p (a n)")
                sg = tmp[:, 4:8, :].rearrange("p a n -> p (a n)")
                act.activation(mag, tab["A2"][:, :], ACT.Sqrt).then_inc(tab_a, 1)
                act.wait_ge(tab_a, wb * TA + 1)
                act.activation(sg, mag, ACT.Sigmoid).then_inc(tab_a, 1)

            def body(wb, b, pair, sblk, u, k):
                par = k % 2
                if k == 0:
                    for src, dst in ((s["rstd"], scale), (s["nmr"], shift)):
                        act.activation(dst[u][:, :], src[:, bass.ds(b, 1)], ACT.Copy).then_inc(scale_set, 1)
                    act.wait_ge(scale_set, (pair * 2 + u) * 2 + 2)
                for j in range(2):
                    act.wait_ge(pe_xT, xTn(sblk, j))
                    act.wait_ge(pe_xn, xnn(sblk, 1, back=2))
                    act.activation(xnT[par][:, 4 * j:4 * j + 4, :].rearrange("p a n -> p (a n)"), pT[:, j, :], ACT.Identity,
                                   bias=shift[u][:, :], scale=scale[u][:, :]
                                   ).then_inc(a_done, 1)
                act.wait_ge(v_done, vn(sblk, "out", back=2))
                for j in range(2):
                    act.wait_ge(pe_z, zn(sblk, j))
                    act.activation(fi[par][:, 4 * j:4 * j + 4, :].rearrange("p a n -> p (a n)"),
                                   pZ[:, 2 * j:2 * j + 2, :].rearrange("p a n -> p (a n)"), ACT.Sigmoid).then_inc(a_done, 1)
                act.wait_ge(pe_z, zn(sblk, 2))
                act.activation(ld[par][:, :], pD[:, :, :].rearrange("p a n -> p (a n)"), ACT.Sigmoid, scale=-1.0).then_inc(a_done, 1)
                act.wait_ge(a_done, an(sblk, "sd"))
                act.activation(ld[par][:, :], ld[par][:, :], ACT.Ln, bias=s["tiny"][:, :]).then_inc(a_done, 1)
                for name, src, dst in (("t", t, tt), ("d", d, d2), ("t2", t2, t2t2), (None, d2, d4), ("t4", t4, t4t4)):
                    if name:
                        act.wait_ge(v_done, vn(sblk, name))
                    act.wait_ge(a_done, an(sblk, "d2")) if name is None else None
                    act.activation(dst, src, ACT.Square).then_inc(a_done, 1)

            blocks(act, tables, body)

        @block.vector
        def _(v):
            v.sem_inc(v_done, 2 * KV)
            v.sem_inc(tab_v, 1)

            def body(wb, b, pair, sblk, u, k):
                par = k % 2
                last = [0]

                def step(name, ins_fn, follows=False):
                    assert V_STEPS[last[0]] == name, name
                    v.wait_ge(v_done, sblk * KV + (2 * KV + last[0] - (0 if follows else 1)))
                    ins_fn().then_inc(v_done, 1)
                    last[0] += 1

                cols = slice(k * HALF, (k + 1) * HALF)

                def both(ap):
                    return view(ap, [CH, SW], [0, 2], [1, CH])

                def w2c(ap):
                    return view(ap, [C, SW], [CH, 2], [1, CH])

                def part(ap, i):
                    return view(ap[:, i * CH:i * CH + 1], [C, SW], [1, CH])

                def h3(ap):
                    return view(ap, [CH, SW], [1, CH])

                Ar, Ai, A2, Br, Bi = (tab[n][:, cols] for n in ("Ar", "Ai", "A2", "Br", "Bi"))
                f_full = fi[par][:, :, 0:C]
                i_full = fi[par][:, :, C:2 * C]
                fr, fim = fi[par][:, :, 0:CH], fi[par][:, :, CH:C]
                xn = pT[:, :, :].rearrange("p a n -> p (a n)")
                tts, tsc = v.tensor_tensor, v.scalar_tensor_tensor
                M1, M2, BX, SP, AV = (z[:, :] for z in (m1, m2, bx, sp_, av))
                if u == 0 and k == 0:
                    v.wait_ge(tab_v, wb * TV + (TV + 1))
                v.wait_ge(pe_xn, xnn(sblk, 1))
                step("m1", lambda: tts(w2c(M1), w2c(xn), both(Br), ALU.mult), True)
                step("m2", lambda: tts(w2c(M2), w2c(xn), both(Bi), ALU.mult))
                v.wait_ge(a_done, an(sblk, "fi1"))
                step("fs", lambda: tts(h3(b1), fr, fim, ALU.add))
                step("p", lambda: tts(h3(a1), fr, fim, ALU.mult))
                step("t", lambda: tts(t, b1, Ar, ALU.mult))
                step("d", lambda: tts(d, a1, A2, ALU.mult))
                v.wait_ge(a_done, an(sblk, "ln"))
                step("sp", lambda: tsc(SP, ld[par][:, :], -1.0, pD[:, :, :].rearrange("p a n -> p (a n)"), ALU.mult, ALU.max))
                step("bxr", lambda: tts(part(BX, 0), part(M1, 0), part(M2, 1), ALU.subtract))
                step("bxi", lambda: tts(part(BX, 1), part(M1, 1), part(M2, 0), ALU.add))
                v.wait_ge(a_done, an(sblk, "tt"))
                step("t2", lambda: tsc(t2, d, -2.0, tt, ALU.mult, ALU.add))
                step("g", lambda: tts(SP.rearrange("p (w c) -> p w c", c=C), SP.rearrange("p (w c) -> p w c", c=C), i_full, ALU.mult))
                step("b1", lambda: tts(b1, t2, d, ALU.mult))
                step("v", lambda: tts(BX, SP, BX, ALU.mult))
                step("a1", lambda: tts(a1, t2, t, ALU.mult))
                v.wait_ge(a_done, an(sblk, "t2t2"))
                step("t4", lambda: tsc(t4, d2, -2.0, t2t2, ALU.mult, ALU.add))
                step("b2", lambda: tts(b1, b1, d2, ALU.add))
                step("s0", lambda: tsc(ss, tt, 1.0, t, ALU.add, ALU.add))
                v.wait_ge(a_done, an(sblk, "d4"))
                step("ep", lambda: tsc(ep, t4, 1.0, d4, ALU.add, ALU.mult))
                v.wait_ge(a_done, an(sblk, "t4t4"))
                step("q0", lambda: tsc(q, t4t4, 1.0, t4, ALU.add, ALU.add))
                step("s", lambda: tts(ss, ss, d, ALU.subtract))
                step("q", lambda: tts(q, q, d4, ALU.subtract))
                step("er", lambda: tsc(er, t, 1.0, d, ALU.add, ALU.mult))
                step("g1", lambda: tts(g1, q, b1, ALU.mult))
                step("y", lambda: tts(y, q, a1, ALU.mult))
                step("negx", lambda: tsc(negx, ep, -1.0, g1, ALU.add, ALU.add))
                step("nry", lambda: tsc(nry, er, -1.0, y, ALU.add, ALU.mult))
                step("rx", lambda: tsc(rx, er, -1.0, negx, ALU.add, ALU.mult))
                step("sy", lambda: tts(ep, ss, y, ALU.mult))
                step("snx", lambda: tts(g1, ss, negx, ALU.mult))
                step("syd", lambda: tts(t2, ep, d, ALU.mult))
                step("syt", lambda: tts(t2t2, ep, t, ALU.mult))
                step("u", lambda: tts(nry, nry, g1, ALU.add))
                step("alpha", lambda: tts(rx, rx, t2, ALU.subtract))
                step("beta", lambda: tts(t2t2, t2t2, nry, ALU.subtract))
                step("w", lambda: tts(w2c(SP), both(t2t2), w2c(BX), ALU.mult), True)
                step("av", lambda: tts(w2c(AV), both(rx), w2c(BX), ALU.mult))
                step("n1", lambda: tts(w2c(M1), w2c(SP), both(Ar), ALU.mult))
                step("n2", lambda: tts(w2c(M2), w2c(SP), both(Ai), ALU.mult))
                step("ax", lambda: tts(AV, AV, xt[u][:, k * SW:(k + 1) * SW, :].rearrange("p w c -> p (w c)"), ALU.add))
                step("mr", lambda: tts(part(SP, 0), part(M1, 0), part(M2, 1), ALU.subtract))
                step("mi", lambda: tts(part(SP, 1), part(M1, 1), part(M2, 0), ALU.add))
                step("fm", lambda: tts(SP.rearrange("p (w c) -> p w c", c=C), SP.rearrange("p (w c) -> p w c", c=C), f_full, ALU.mult), True)
                if k == 0:
                    v.wait_ge(x1_out[u], (pair + 1) * 16)
                step("out", lambda: tts(ot[u][:, :, k * SW:(k + 1) * SW], view(SP, [1, C], [C, SW]),
                                        view(AV, [1, C], [C, SW]), ALU.add), True)
                assert last[0] == KV

            def build_tables(wb):
                count = [0]

                def step(ins, wait=True):
                    ins.then_inc(tab_v, 1)
                    count[0] += 1
                    if wait:
                        v.wait_ge(tab_v, wb * TV + (1 + count[0]))

                mag, sg, rc = (tmp[:, 4 * i:4 * i + 4, :].rearrange("p a n -> p (a n)") for i in range(3))
                Ar, Ai, A2 = tab["Ar"][:, :], tab["Ai"][:, :], tab["A2"][:, :]
                v.wait_ge(v_done, vn(wb * (B * SUBS), "out", back=1))
                for j in range(4):
                    v.wait_ge(tab_pe, wb * 4 + (2 + j))
                    for i, name in enumerate(("Ar", "Ai", "Br", "Bi")):
                        step(v.tensor_scalar(tab[name][:, j * HALF:(j + 1) * HALF].rearrange("p (w c) -> p w c", c=CH),
                                             view(pZ[:, 0, i * CH:i * CH + 1], [256, SW], [1, CH]),
                                             1.0 if i < 2 else 0.1, None, ALU.mult), wait=i == 3)
                step(v.tensor_tensor(rc, Ai, Ai, ALU.mult), wait=False)
                step(v.tensor_tensor(A2, Ar, Ar, ALU.mult))
                step(v.scalar_tensor_tensor(A2, A2, 1e-8, rc, ALU.add, ALU.add))
                v.wait_ge(tab_a, wb * TA + 2)
                step(v.tensor_scalar(mag, mag, 1e-8, None, ALU.add))
                step(v.reciprocal(rc, mag))
                step(v.scalar_tensor_tensor(rc, sg, 0.95, rc, ALU.mult, ALU.mult))
                step(v.tensor_tensor(Ar, Ar, rc, ALU.mult), wait=False)
                step(v.tensor_tensor(Ai, Ai, rc, ALU.mult))
                step(v.tensor_tensor(rc, Ai, Ai, ALU.mult), wait=False)
                step(v.tensor_tensor(A2, Ar, Ar, ALU.mult))
                step(v.tensor_tensor(A2, A2, rc, ALU.add), wait=False)
                assert count[0] == TV

            blocks(v, build_tables, body)


def channel_steps(last):
    dve, act = [], []
    for cc in range(CG):
        prep = not (last and cc == CG - 1)
        if not last and cc == 3:
            dve += ["mean", "de", "do", "m2", "dq", "ds", "vs", "ve", "rs"]
            act += ["sq"]
        if prep:
            dve += [f"{n}{cc}" for n in ("xs", "xm", "hl", "hr", "xl", "tl")]
            act += [f"{n}{cc}" for n in ("xh", "th")]
        act += [f"{n}{cc}" for n in ("z0_", "z1_", "z2_", "z3_", "ga")]
        if not last and cc == 2:
            dve += [f"bn{b}" for b in range(B)]
        dve += [f"{n}{cc}" for n in ("at", "c2_", "c4_", "f0_", "f1_", "f2_", "bt0_", "bt1_", "bt2_", "bt3_", "sp", "o", "oa", "ob")]
        act += [f"{n}{cc}" for n in ("s1_", "c1_", "sb", "ln")]
    return dve, act


def layer1_conv(nc, x1, hs, rows_dram, s):
    XW = W + 10
    with ExitStack() as ctx:
        def sb(name, shape, dt=F32):
            return ctx.enter_context(nc.sbuf_tensor(name, shape, dt))

        def sem(name):
            return ctx.enter_context(nc.semaphore(name))

        NQ = 3 * TAPS
        xg = sb("xg", [P, B, NWB, CG, WB])
        traw = [sb(f"traw{i}", [P, NQ, P]) for i in range(2)]
        thi = [sb(f"thi{i}", [P, 2 * TAPS, P], F32R) for i in range(2)]
        tlo = [sb(f"tlo{i}", [P, 2 * TAPS, P], F32R) for i in range(2)]
        xn = [sb(f"xn{i}", [P, B, XW]) for i in range(2)]
        xhi = [sb(f"xhi{i}", [P, B, XW], F32R) for i in range(2)]
        xlo = [sb(f"xlo{i}", [P, B, XW], F32R) for i in range(2)]
        og = sb("og", [P, B, NWB, CG, WB])
        gate = sb("gate", [P, B * W])
        bt = sb("bt", [P, B * W])
        lns = sb("lns", [P, B * W])
        st = sb("st1", [P, B, 6])
        mean = sb("mean1", [P, B])
        rstd = sb("rstd1", [P, B])
        dev = sb("dev1", [P, 2, B])
        vs = sb("vs1", [P, B])
        ve = sb("ve1", [P, B])
        sq = sb("sq1", [P, B])
        sga, at, s1, c1, c2, c4, ff = (sb(n, [P, B, 8]) for n in ("sga", "at", "s1", "c1", "c2", "c4", "ff"))
        pG = ctx.enter_context(nc.psum_tensor("pG", [P, 4, 512], F32))
        pB = ctx.enter_context(nc.psum_tensor("pB", [P, 4, 512], F32))
        pe_zg, pe_zb, pe_ga, pe_mean, pe_var = (sem(n) for n in ("pe_zg", "pe_zb", "pe_ga", "pe_mean", "pe_var"))
        v_done, a_done = sem("cv_done"), sem("ca_done")
        xg_in, t_in = sem("xg_in"), [sem(f"t_in{i}") for i in range(2)]
        hs_out = sem("hs_out")
        first_v, first_a, first_p = sem("first_v"), sem("first_a"), sem("first_p")
        block = ctx.enter_context(nc.Block())

        names = {last: channel_steps(last) for last in (False, True)}
        place = {last: [{n: i + 1 for i, n in enumerate(x)} for x in names[last]] for last in (False, True)}
        KV1, KA1 = (len(x) for x in names[False])

        def vc(g, name, last=False, back=0):
            return g * KV1 + ((1 - back) * KV1 + place[last][0][name])

        def ac(g, name, last=False, back=0):
            return g * KA1 + ((1 - back) * KA1 + place[last][1][name])

        def chan(g, cc):
            return g * CG + (cc + 2)

        def groups(eng, do):
            with eng.Fori(0, G // 2 - 1) as i:
                for gp in range(2):
                    do(i * 2 + gp, False)
            do(G - 2, False)
            do(G - 1, True)

        @block.sync
        def _(sp):
            sp.sem_inc(hs_out, 16)

            def load_group(g):
                src = x1[g] if isinstance(g, int) else x1[bass.ds(g, 1)].rearrange("a h b e c w -> (a h) b e c w")
                sp.dma_start(xg[:, :, :, :, :].rearrange("p b e c w -> p (b e c w)"),
                             src.rearrange("h b e c w -> h (b e c w)")).then_inc(xg_in, 16)

            def load_taps(c, par):
                base = rows_dram[bass.ds(c, 1), :]
                src = bass.AP(base.tensor, base.offset, [[1, P], [256, NQ], [1, P]])
                sp.dma_start(traw[par][:, :, :], src).then_inc(t_in[par], 16)

            load_group(0)
            for i in range(2):
                load_taps(i, i)

            def do(g, last):
                for cc in range(CG):
                    if cc == 2 and not last:
                        sp.wait_ge(v_done, vc(g, "hr2"))
                        load_group(g + 1)
                    if not (last and cc >= 2):
                        sp.wait_ge(pe_ga, chan(g, cc) + 1)
                        load_taps(g * CG + (cc + 2), cc % 2)
                sp.wait_ge(v_done, vc(g, "ob3", last))
                dst = (hs[g] if isinstance(g, int) else hs[bass.ds(g, 1)].rearrange("a h b e c w -> (a h) b e c w"))
                sp.dma_start(dst.rearrange("h b e c w -> h (b e c w)"),
                             og[:, :, :, :, :].rearrange("p b e c w -> p (b e c w)")).then_inc(hs_out, 16)

            groups(sp, do)
            sp.wait_ge(hs_out, 16 * (G + 1))

        @block.tensor
        def _(pe):
            pe.sem_inc(pe_zg, 8)
            pe.sem_inc(pe_zb, 8)
            pe.sem_inc(pe_ga, 2)
            pe.sem_inc(pe_mean, 1)
            pe.sem_inc(pe_var, 1)

            def mean_mm():
                pe.matmul(pB[:, 0, 0:B], s["ones_n"][:, :], st[:, :, 1], start=True, stop=False)
                return pe.matmul(pB[:, 0, 0:B], s["ones_n"][:, :], st[:, :, 4], start=False, stop=True)

            def var_mm():
                return pe.matmul(pB[:, 0, 0:B], s["ones_n"][:, :], vs[:, :], start=True, stop=True)

            pe.wait_ge(first_v, B)
            mean_mm().then_inc(first_p, 1)
            pe.wait_ge(first_v, B + 7)
            var_mm().then_inc(first_p, 1)

            def conv(ps, q0, par, taps):
                last = []
                for j in taps:
                    for t, xs in ((thi, xhi), (thi, xlo), (tlo, xhi)):
                        for k in range(4):
                            fin = j == TAPS - 1 and t is tlo
                            m = pe.matmul(ps[:, k, :], t[par][:, q0 + j, :],
                                          xs[par][:, 4 * k:4 * k + 4, 10 - j:10 - j + W],
                                          start=j == 0 and xs is xhi and t is thi, stop=fin)
                            if fin:
                                last.append(m)
                return last

            def do(g, last):
                for cc in range(CG):
                    par = cc % 2
                    if cc == 0:
                        pe.wait_ge(v_done, vc(g, "tl3", back=1))
                        pe.wait_ge(a_done, ac(g, "ga3", back=1))
                    else:
                        pe.wait_ge(v_done, vc(g, f"tl{cc - 1}", last))
                        pe.wait_ge(a_done, ac(g, f"ga{cc - 1}", last))
                    conv(pG, 0, par, range(3))
                    if cc == 3 and not last:
                        pe.wait_ge(v_done, vc(g, "bt3_2"))
                        mean_mm().then_inc(pe_mean, 1)
                    conv(pG, 0, par, range(3, 5))
                    if cc == 3 and not last:
                        pe.wait_ge(v_done, vc(g, "vs"))
                        var_mm().then_inc(pe_var, 1)
                    for m in conv(pG, 0, par, range(5, TAPS)):
                        m.then_inc(pe_zg, 1)
                    if cc == 3 and not last:
                        pe.wait_ge(v_done, vc(g, "ve"))
                    pe.wait_ge(v_done, vc(g, "bt3_3", back=1) if cc == 0 else vc(g, f"bt3_{cc - 1}", last))
                    conv(pB, TAPS, par, range(3))
                    pe.wait_ge(a_done, ac(g, f"z0_{cc}", last))
                    for j in range(TAPS):
                        m = pe.matmul(pG[:, 0, 0:B * 8], traw[par][:, 2 * TAPS + j, :],
                                      xn[par][:, :, 6 - j:6 - j + 8], start=j == 0, stop=j == TAPS - 1)
                    m.then_inc(pe_ga, 1)
                    for m in conv(pB, TAPS, par, range(3, TAPS)):
                        m.then_inc(pe_zb, 1)

            groups(pe, do)

        @block.scalar
        def _(act):
            def split(par, tick):
                tick("xh", lambda: act.activation(xhi[par][:, :, :].rearrange("p b w -> p (b w)"),
                                                  xn[par][:, :, :].rearrange("p b w -> p (b w)"), ACT.Copy))
                tick("th", lambda: act.activation(thi[par][:, :, :].rearrange("p q m -> p (q m)"),
                                                  traw[par][:, 0:2 * TAPS, :].rearrange("p q m -> p (q m)"), ACT.Copy))

            act.wait_ge(first_v, B + 8)
            act.activation(sq[:, :], ve[:, :], ACT.Sqrt).then_inc(first_a, 1)
            act.wait_ge(first_v, B + 13)
            act.wait_ge(t_in[0], 16)
            split(0, lambda name, f: f().then_inc(first_a, 1))
            act.sem_inc(a_done, KA1)

            def do(g, last):
                for cc in range(CG):
                    nxt = (cc + 1) % 2

                    def step(name, f):
                        f().then_inc(a_done, 1)

                    if cc == 3 and not last:
                        act.wait_ge(v_done, vc(g, "ve"))
                        step("sq", lambda: act.activation(sq[:, :], ve[:, :], ACT.Sqrt))
                    if not (last and cc == CG - 1):
                        act.wait_ge(v_done, vc(g, f"hr{cc}", last))
                        act.wait_ge(pe_zb, chan(g, cc) * 4)
                        act.wait_ge(t_in[nxt], (g * 2 + (1 + (cc + 1) // 2)) * 16)
                        split(nxt, step)
                    for k in range(4):
                        act.wait_ge(pe_zg, chan(g, cc) * 4 + (k + 1))
                        if k == 0:
                            act.wait_ge(v_done, vc(g, "bt3_3", back=1) if cc == 0 else vc(g, f"bt3_{cc - 1}", last))
                        step("z", lambda: act.activation(gate[:, k * 512:(k + 1) * 512], pG[:, k, :], ACT.Sigmoid))
                    act.wait_ge(pe_ga, chan(g, cc) + 1)
                    step("ga", lambda: act.activation(sga[:, :, :].rearrange("p b w -> p (b w)"), pG[:, 0, 0:B * 8], ACT.Sigmoid))
                    act.wait_ge(v_done, vc(g, f"at{cc}", last))
                    step("s1", lambda: act.activation(s1[:, :, :], at[:, :, :], ACT.Sigmoid))
                    step("c1", lambda: act.activation(c1[:, :, :], at[:, :, :], ACT.Sigmoid, scale=-1.0))
                    act.wait_ge(v_done, vc(g, f"bt3_{cc}", last))
                    step("sb", lambda: act.activation(lns[:, :], bt[:, :], ACT.Sigmoid, scale=-1.0))
                    act.wait_ge(a_done, ac(g, f"sb{cc}", last))
                    step("ln", lambda: act.activation(lns[:, :], lns[:, :], ACT.Ln, bias=s["tiny"][:, :]))

            groups(act, do)

        @block.vector
        def _(v):
            tts, tsc = v.tensor_tensor, v.scalar_tensor_tensor

            def bn(b):
                return v.bn_stats(st[:, b, :], xg[:, b, :, :, :].rearrange("p e c w -> p (e c w)"))

            def stats_mid():
                yield "mean", lambda: v.tensor_copy(mean[:, :], pB[:, 0, 0:B])
                yield "de", lambda: tts(dev[:, 0, :], st[:, :, 1], pB[:, 0, 0:B], ALU.subtract)
                yield "do", lambda: tts(dev[:, 1, :], st[:, :, 4], pB[:, 0, 0:B], ALU.subtract)
                yield "m2", lambda: tts(vs[:, :], st[:, :, 2], st[:, :, 5], ALU.add)
                yield "dq", lambda: tts(dev[:, :, :], dev[:, :, :], dev[:, :, :], ALU.mult)
                yield "ds", lambda: tts(dev[:, 0, :], dev[:, 0, :], dev[:, 1, :], ALU.add)
                yield "vs", lambda: tsc(vs[:, :], vs[:, :], 1.0 / (W * CG // 2), dev[:, 0, :], ALU.mult, ALU.add)

            def ve_():
                return v.tensor_scalar(ve[:, :], pB[:, 0, 0:B], GN_EPS, None, ALU.add)

            def rs_():
                return v.reciprocal(rstd[:, :], sq[:, :])

            def norm(cc, par, step):
                src = view(xg[:, 0, 0, cc, 0:1], [NWB * CG * WB, B], [CG * WB, NWB], [1, WB])
                mid = view(xn[par][:, 0, 7:8], [XW, B], [WB, NWB], [1, WB])
                step("xs", lambda: tts(mid, src, view(mean[:, 0:1], [1, B], [0, NWB], [0, WB]), ALU.subtract))
                step("xm", lambda: tts(xn[par][:, :, 7:7 + W], xn[par][:, :, 7:7 + W],
                                       view(rstd[:, 0:1], [1, B], [0, W]), ALU.mult))
                step("hl", lambda: v.tensor_copy(xn[par][:, :, 0:7], xn[par][:, :, W:W + 7]))
                step("hr", lambda: v.tensor_copy(xn[par][:, :, W + 7:W + 10], xn[par][:, :, 7:10]))

            def low(par, step):
                step("xl", lambda: tts(xlo[par][:, :, :], xn[par][:, :, :], xhi[par][:, :, :].bitcast(F32), ALU.subtract))
                step("tl", lambda: tts(tlo[par][:, :, :], traw[par][:, 0:2 * TAPS, :], thi[par][:, :, :].bitcast(F32), ALU.subtract))

            n = [0]

            def first(name, f):
                f().then_inc(first_v, 1)
                n[0] += 1
                v.wait_ge(first_v, n[0])

            v.wait_ge(xg_in, 16)
            for b in range(B):
                first("bn", lambda: bn(b))
            v.wait_ge(first_p, 1)
            for name, f in stats_mid():
                first(name, f)
            v.wait_ge(first_p, 2)
            first("ve", ve_)
            v.wait_ge(first_a, 1)
            first("rs", rs_)
            norm(0, 0, first)
            v.wait_ge(first_a, 3)
            low(0, first)
            assert n[0] == B + 15
            v.sem_inc(v_done, KV1)

            def do(g, last):
                done = [0]
                order = names[last][0]

                def step(name, f, follows=True):
                    assert order[done[0]] == name, (order[done[0]], name)
                    v.wait_ge(v_done, g * KV1 + (KV1 + done[0] - (0 if follows else 1)))
                    f().then_inc(v_done, 1)
                    done[0] += 1

                for cc in range(CG):
                    par, nxt = cc % 2, (cc + 1) % 2
                    if cc == 3 and not last:
                        v.wait_ge(pe_mean, g + 2)
                        for name, f in stats_mid():
                            step(name, f)
                        v.wait_ge(pe_var, g + 2)
                        step("ve", ve_)
                        v.wait_ge(a_done, ac(g, "sq"))
                        step("rs", rs_)
                    if not (last and cc == CG - 1):
                        v.wait_ge(pe_ga, chan(g, cc))
                        norm((cc + 1) % CG, nxt, lambda name, f: step(f"{name}{cc}", f))
                        v.wait_ge(a_done, ac(g, f"th{cc}", last))
                        low(nxt, lambda name, f: step(f"{name}{cc}", f))
                    if cc == 2 and not last:
                        v.wait_ge(xg_in, g * 16 + 32)
                        for b in range(B):
                            step(f"bn{b}", lambda: bn(b), False)
                    c = g * CG + cc
                    v.wait_ge(a_done, ac(g, f"ga{cc}", last))
                    step(f"at{cc}", lambda: tts(at[:, :, :], sga[:, :, :], apad_of(c), ALU.mult))
                    v.wait_ge(a_done, ac(g, f"c1_{cc}", last))
                    step(f"c2_{cc}", lambda: tts(c2[:, :, :], c1[:, :, :], c1[:, :, :], ALU.mult))
                    step(f"c4_{cc}", lambda: tts(c4[:, :, :], c2[:, :, :], c2[:, :, :], ALU.mult))
                    fl = [z[:, :, :].rearrange("p b w -> p (b w)") for z in (ff, c1, c2, c4, s1)]
                    step(f"f0_{cc}", lambda: tsc(fl[0], fl[1], 1.0, fl[4], ALU.add, ALU.mult))
                    step(f"f1_{cc}", lambda: tsc(fl[0], fl[2], 1.0, fl[0], ALU.add, ALU.mult))
                    step(f"f2_{cc}", lambda: tsc(fl[0], fl[3], 1.0, fl[0], ALU.add, ALU.mult))
                    for k in range(4):
                        v.wait_ge(pe_zb, chan(g, cc) * 4 + (k + 1))
                        step(f"bt{k}_{cc}", lambda: tts(bt[:, k * 512:(k + 1) * 512], gate[:, k * 512:(k + 1) * 512], pB[:, k, :], ALU.mult), False)
                    v.wait_ge(a_done, ac(g, f"ln{cc}", last))
                    step(f"sp{cc}", lambda: tsc(bt[:, :], lns[:, :], -1.0, bt[:, :], ALU.mult, ALU.max))
                    if cc == 0:
                        v.wait_ge(hs_out, g * 16 + 16)
                    step(f"o{cc}", lambda: v.tensor_scalar(view(og[:, 0, 0, cc, 0:1], [NWB * CG * WB, B], [CG * WB, NWB], [1, WB]),
                                                           bt[:, :].rearrange("p (b e w) -> p b e w", b=B, e=NWB), 1e-6, 255.0 / 256.0, ALU.add, ALU.mult))
                    step(f"oa{cc}", lambda: tsc(og[:, :, NWB - 1, cc, WB - 4:WB], view(bt[:, W - 4:W - 3], [W, B], [1, 4]), 1e-6, ff[:, :, 0:4], ALU.add, ALU.mult))
                    step(f"ob{cc}", lambda: tsc(og[:, :, 0, cc, 0:4], view(bt[:, 0:1], [W, B], [1, 4]), 1e-6, ff[:, :, 4:8], ALU.add, ALU.mult))
                assert done[0] == len(order)

            def apad_of(c):
                a = s["apad"][:, c, :] if isinstance(c, int) else s["apad"][:, bass.ds(c, 1), :]
                return view(a, [0, B], [1, 8])

            groups(v, do)


def layer1_out(nc, x1, hs, y, s):
    with ExitStack() as ctx:
        def sb(name, shape, dt=F32):
            return ctx.enter_context(nc.sbuf_tensor(name, shape, dt))

        def sem(name):
            return ctx.enter_context(nc.semaphore(name))

        ht = [sb(f"ht{i}", [P, C, WB]) for i in range(2)]
        xt = [sb(f"x1t{i}", [P, C, WB]) for i in range(2)]
        yt = [sb(f"yt{i}", [P, WB, C]) for i in range(2)]
        hT = [sb(f"hT{i}", [P, 4, P]) for i in range(2)]
        pT = [ctx.enter_context(nc.psum_tensor(f"dT{i}", [P, 512], F32)) for i in range(2)]
        pO = [ctx.enter_context(nc.psum_tensor(f"dO{i}", [P, 512], F32)) for i in range(2)]
        NQD = WB // 4
        h_in, x_in, y_out = ([sem(f"{n}{i}") for i in range(2)] for n in ("h_in", "x1_in", "y_out"))
        pe_T, pe_O, a_done, v_done = sem("pe_T"), sem("pe_O"), sem("da_done"), sem("dv_done")
        block = ctx.enter_context(nc.Block())

        def tiles(eng, body):
            with eng.Fori(0, NWB) as wb:
                with eng.Fori(0, B // 2) as ip:
                    for u in range(2):
                        for k in range(NQD):
                            body(wb * (B // 2) + ip, (wb * B + ip * 2 + u) * NQD + k, u, k)

        @block.sync
        def _(sp):
            for u in range(2):
                sp.sem_inc(y_out[u], 16)
            with sp.Fori(0, NWB) as wb:
                def load(b, u):
                    for src, dst, sm in ((hs, ht, h_in), (x1, xt, x_in)):
                        sp.dma_start(dst[u][:, :, :].rearrange("p (g c) w -> p g (c w)", g=G),
                                     src[:, :, bass.ds(b, 1), bass.ds(wb, 1), :, :].rearrange("g h a e c w -> h g (a e c w)")
                                     ).then_inc(sm[u], 16)

                def store(b, u):
                    sp.wait_ge(v_done, (wb * B + b) * NQD + (2 + NQD))
                    sp.dma_start(y[bass.ds(b, 1), :, bass.ds(wb * WB, WB), :].rearrange("a h w c -> (a h) (w c)"),
                                 yt[u][:, :, :].rearrange("p w c -> p (w c)")).then_inc(y_out[u], 16)

                for u in range(2):
                    load(u, u)
                with sp.Fori(0, B // 2 - 1) as ip:
                    for u in range(2):
                        store(ip * 2 + u, u)
                        load(ip * 2 + (2 + u), u)
                for u in range(2):
                    store(B - 2 + u, u)
            for u in range(2):
                sp.wait_ge(y_out[u], 16 * (TILES // 2 + 1))

        @block.tensor
        def _(pe):
            pe.sem_inc(pe_O, 2)

            def body(pair, n, u, k):
                r = k % 2
                if k == 0:
                    pe.wait_ge(h_in[u], (pair + 1) * 16)
                pe.wait_ge(a_done, n + 1)
                for w in range(4):
                    last = pe.transpose(pT[r][:, w * P:(w + 1) * P], ht[u][:, :, 4 * k + w], s["ident"][:, :])
                last.then_inc(pe_T, 1)
                pe.wait_ge(v_done, n + 1)
                pe.matmul(pO[r][:, :], s["ones3"][0:3, :], s["b_o"][0:3, :, :], start=True, stop=False)
                pe.wait_ge(a_done, n + 3)
                for w in range(4):
                    last = pe.matmul(pO[r][:, w * C:(w + 1) * C], hT[r][:, w, :], s["wout"][:, :], start=False, stop=w == 3)
                last.then_inc(pe_O, 1)

            tiles(pe, body)

        @block.scalar
        def _(act):
            act.sem_inc(a_done, 2)

            def body(pair, n, u, k):
                r = k % 2
                act.wait_ge(pe_T, n + 1)
                act.wait_ge(pe_O, n + 1)
                act.activation(view(hT[r][:, 0, P - 1:P], [P, 4], [-1, P]),
                               pT[r][:, :].rearrange("p (w h) -> p w h", h=P), ACT.Copy).then_inc(a_done, 1)

            tiles(act, body)

        @block.vector
        def _(v):
            v.sem_inc(v_done, 2)

            def body(pair, n, u, k):
                r = k % 2
                if k == 0:
                    v.wait_ge(x_in[u], (pair + 1) * 16)
                    v.wait_ge(y_out[u], (pair + 1) * 16)
                v.wait_ge(pe_O, n + 3)
                v.tensor_tensor(yt[u][:, 4 * k:4 * k + 4, :], view(xt[u][:, 0, 4 * k:4 * k + 1], [1, 4], [WB, C]),
                                pO[r][:, :].rearrange("p (w c) -> p w c", c=C), ALU.add).then_inc(v_done, 1)

            tiles(v, body)


PHASES = 4


def build(nc, d, y):
    with ExitStack() as ctx:
        def sb(name, shape, dt=F32):
            return ctx.enter_context(nc.sbuf_tensor(name, shape, dt))

        s = {
            "ident": sb("ident", [P, P]), "mask": sb("mask", [C, G]), "ones_n": sb("ones_n", [P, P]),
            "ones3": sb("ones3", [3, P], BF16), "tiny": sb("tiny", [P, 1]),
            "wfi": sb("wfi", [C, 2 * C]), "wd": sb("wd", [C, C]), "wout": sb("wout", [C, C]),
            "km": sb("km", [2 * TAPS * TAPS, 4 * CH]), "b_fi": sb("b_fi", [3, 2, 2 * C], BF16),
            "b_d": sb("b_d", [3, 4, C], BF16), "b_o": sb("b_o", [3, 4, C], BF16),
            "apad": sb("apad", [P, C, 8]), "rstd": sb("rstd", [C, B]), "nmr": sb("nmr", [C, B]),
        }
        rows_dram = nc.dram_tensor("rows_dram", (C, 3 * TAPS * 256), F32).ap()
        x1 = nc.dram_tensor("x1", (G, H, B, NWB, CG, WB), F32).ap()
        hs = nc.dram_tensor("hs", (G, H, B, NWB, CG, WB), F32).ap()
        setup(nc, d, s, rows_dram)
        stats_of_x(nc, d["x"], s["rstd"], s["nmr"], s["ones_n"], s["mask"])
        layer0(nc, d["x"], x1, d["basis"], s)
        layer1_conv(nc, x1, hs, rows_dram, s)
        layer1_out(nc, x1, hs, y, s)


def constants():
    i = np.arange(TAPS) + (H - TAPS) // 2
    kw, kh = np.arange(W), np.arange(H)
    ang = 2 * np.pi * ((kh[None, None, None, :] * i[:, None, None, None]
                        + kw[None, None, :, None] * i[None, :, None, None]) % H) / H
    ang = ang.reshape(TAPS * TAPS, W, H)
    basis = np.concatenate([np.cos(ang), np.sin(ang)]).astype(np.float32)
    sign = np.ones((2 * TAPS * TAPS, 4 * CH), np.float32)
    sign[TAPS * TAPS:, CH:2 * CH] = -1
    sign[TAPS * TAPS:, 3 * CH:] = -1
    mask = (np.arange(C)[:, None] // CG == np.arange(G)[None]).astype(np.float32)
    return {"basis": basis, "km_sign": sign, "ident": np.eye(P, dtype=np.float32), "mask": mask}


def kernel(**inputs):
    import concourse.bacc as bacc
    from concourse.bass_utils import run_bass_kernel_spmd

    a = {k: np.asarray(v) for k, v in inputs.items()}

    def taps_first(k):
        return np.transpose(k.reshape(k.shape[0], -1))

    ar, ai, br, bi = (taps_first(a[f"L0_conv_{n}"]) for n in ("A_real", "A_imag", "B_real", "B_imag"))
    km = np.concatenate([np.concatenate([ar, ai, br, bi], 1), np.concatenate([ai, ar, bi, br], 1)], 0)
    taps = np.stack([np.transpose(a[f"L1_conv_{n}"], (0, 2, 1))[:, :, ::-1] for n in ("gate_B_kernel", "B_kernel", "gate_A_kernel")], 1)
    apad = np.zeros((P, C, 8), np.float32)
    apad[H - 1 - (np.arange(TAPS) - TAPS // 2) % H, :, 1:] = np.transpose(a["L1_conv_A_kernel"], (1, 0, 2))
    arrays = {
        "x": a["x"], "Wf": a["L0_conv_Wf"], "Wi": a["L0_conv_Wi"], "Wd": a["L0_conv_Wd"], "W_out": a["L1_conv_W_out"],
        "bf": a["L0_conv_bf"][None], "bi": a["L0_conv_bi"][None], "bd": a["L0_conv_bd"][None], "b_out": a["L1_conv_b_out"][None],
        "km": km, "taps": taps.reshape(C, 3 * TAPS, TAPS), "apad": apad, **constants(),
    }
    arrays = {f"in_{k}": np.ascontiguousarray(v) for k, v in arrays.items()}
    nc = bacc.Bacc("TRN2", target_bir_lowering=False, num_devices=1)
    d = {k[3:]: nc.dram_tensor(k, v.shape, mybir.dt.from_np(v.dtype), kind="ExternalInput").ap() for k, v in arrays.items()}
    y = nc.dram_tensor("out_y", (B, H, W, C), F32, kind="ExternalOutput").ap()
    build(nc, d, y)
    r = run_bass_kernel_spmd(nc, [arrays], core_ids=[0])
    return r.results[0]["out_y"]
```

```python
from contextlib import ExitStack

import numpy as np
import concourse.bass as bass
from concourse import mybir

F32 = mybir.dt.float32
F32R = mybir.dt.float32r
BF16 = mybir.dt.bfloat16
ALU = mybir.AluOpType
ACT = mybir.ActivationFunctionType
AX = mybir.AxisListType

P = 128
B, H, W, C = 16, 128, 128, 128
CH = C // 2
TAPS = 7
G = 32
CG = C // G
WB = 32
NWB = W // WB
TILES = NWB * B
SW = 8
SUBS = WB // SW
HALF = SW * CH
FULL = SW * C
GN_EPS = 1e-5
TINY = 2.0 ** -63


def view(ap, *dims):
    return bass.AP(ap.tensor, ap.offset, [list(ap.ap[0])] + [list(d) for d in dims])


def stats_of_x(nc, x, rstd_c, nmr_c, ones_n, mask):
    NPX = B * G
    with ExitStack() as ctx:
        img = [ctx.enter_context(nc.sbuf_tensor(f"img{i}", [P, W * C], F32)) for i in range(2)]
        st = ctx.enter_context(nc.sbuf_tensor("xst", [P, B, G, 6], F32))
        dev = ctx.enter_context(nc.sbuf_tensor("xdev", [P, 2, NPX], F32))
        m2 = ctx.enter_context(nc.sbuf_tensor("xm2", [P, NPX], F32))
        mean = ctx.enter_context(nc.sbuf_tensor("xmean", [P, NPX], F32))
        sd = ctx.enter_context(nc.sbuf_tensor("xsd", [P, NPX], F32))
        rs = ctx.enter_context(nc.sbuf_tensor("xrs", [P, NPX], F32))
        mps = ctx.enter_context(nc.psum_tensor("xmean_ps", [P, NPX], F32))
        vps = ctx.enter_context(nc.psum_tensor("xvar_ps", [P, NPX], F32))
        img_in = [ctx.enter_context(nc.semaphore(f"img_in{i}")) for i in range(2)]
        counted = ctx.enter_context(nc.semaphore("counted"))
        mean_ready = ctx.enter_context(nc.semaphore("mean_ready"))
        var_ready = ctx.enter_context(nc.semaphore("var_ready"))
        sd_ready = ctx.enter_context(nc.semaphore("sd_ready"))
        steps = ctx.enter_context(nc.semaphore("xsteps"))
        block = ctx.enter_context(nc.Block())

        @block.sync
        def _(sp):
            for u in range(2):
                sp.dma_start(img[u][:, :], x[u].rearrange("h w c -> h (w c)")).then_inc(img_in[u], 16)
            with sp.Fori(0, B // 2 - 1) as i:
                for u in range(2):
                    sp.wait_ge(counted, (i * 2 + (u + 1)) * G)
                    src = x[bass.ds(i * 2 + (2 + u), 1)].rearrange("a h w c -> (a h) (w c)")
                    sp.dma_start(img[u][:, :], src).then_inc(img_in[u], 16)

        @block.vector
        def _(v):
            with v.Fori(0, B // 2) as i:
                for u in range(2):
                    v.wait_ge(img_in[u], (i + 1) * 16)
                    for g in range(G):
                        v.bn_stats(st[:, bass.ds(i * 2 + u, 1), g, :],
                                   view(img[u][:, g * CG:g * CG + 1], [C, W], [1, CG])).then_inc(counted, 1)
            n = [0]

            def step(ins):
                ins.then_inc(steps, 1)
                n[0] += 1
                v.wait_ge(steps, n[0])

            fl = st[:, :, :, :].rearrange("p b g s -> p (b g) s")
            v.wait_ge(mean_ready, 1)
            step(v.tensor_tensor(dev[:, 0, :], fl[:, :, 1], mps[:, :], ALU.subtract))
            step(v.tensor_tensor(dev[:, 1, :], fl[:, :, 4], mps[:, :], ALU.subtract))
            step(v.tensor_copy(mean[:, :], mps[:, :]))
            step(v.tensor_tensor(m2[:, :], fl[:, :, 2], fl[:, :, 5], ALU.add))
            step(v.tensor_tensor(dev[:, :, :], dev[:, :, :], dev[:, :, :], ALU.mult))
            step(v.tensor_tensor(dev[:, 0, :], dev[:, 0, :], dev[:, 1, :], ALU.add))
            step(v.scalar_tensor_tensor(dev[:, 0, :], m2[:, :], 1.0 / (W * CG // 2), dev[:, 0, :],
                                        ALU.mult, ALU.add))
            v.wait_ge(var_ready, 1)
            step(v.tensor_scalar(m2[:, :], vps[:, :], GN_EPS, None, ALU.add))
            v.wait_ge(sd_ready, 1)
            step(v.reciprocal(rs[:, :], sd[:, :]))
            step(v.scalar_tensor_tensor(mean[:, :], mean[:, :], -1.0, rs[:, :], ALU.mult, ALU.mult))
            for src, dst in ((rs, rstd_c), (mean, nmr_c)):
                step(v.tensor_tensor(dev[:, 0, :].rearrange("p (b g) -> p b g", g=G),
                                     src[:, :].rearrange("p (b g) -> p b g", g=G),
                                     view(mask[:, 0:1], [0, B], [1, G]), ALU.mult))
                step(v.reduce_sum(dst[:, :], dev[:, 0, :].rearrange("p (b g) -> p b g", g=G), axis=AX.X))

        @block.tensor
        def _(pe):
            fl = st[:, :, :, :].rearrange("p b g s -> p (b g) s")
            pe.wait_ge(counted, B * G)
            pe.matmul(mps[:, :], ones_n[:, :], fl[:, :, 1], start=True, stop=False)
            pe.matmul(mps[:, :], ones_n[:, :], fl[:, :, 4], start=False, stop=True).then_inc(mean_ready, 1)
            pe.wait_ge(steps, 7)
            pe.matmul(vps[:, :], ones_n[:, :], dev[:, 0, :], start=True, stop=True).then_inc(var_ready, 1)

        @block.scalar
        def _(act):
            act.wait_ge(steps, 8)
            act.activation(sd[:, :], m2[:, :], ACT.Sqrt).then_inc(sd_ready, 1)


def setup(nc, d, s, rows_dram):
    with ExitStack() as ctx:
        raw = ctx.enter_context(nc.sbuf_tensor("bias_raw", [1, 4, C], F32))
        rest = ctx.enter_context(nc.sbuf_tensor("bias_rest", [1, 4, C], F32))
        parts = ctx.enter_context(nc.sbuf_tensor("bias_parts", [1, 3, 4, C], BF16))
        kmraw = ctx.enter_context(nc.sbuf_tensor("km_raw", [2 * TAPS * TAPS, 4 * CH], F32))
        kmsign = ctx.enter_context(nc.sbuf_tensor("km_sign", [2 * TAPS * TAPS, 4 * CH], F32))
        taps = ctx.enter_context(nc.sbuf_tensor("taps", [C, 3 * TAPS, TAPS], F32))
        rows = ctx.enter_context(nc.sbuf_tensor("rows", [C, 3 * TAPS, 256], F32))
        loaded = ctx.enter_context(nc.semaphore("consts_in"))
        steps = ctx.enter_context(nc.semaphore("setup_steps"))
        placed = ctx.enter_context(nc.semaphore("parts_placed"))
        rows_out = ctx.enter_context(nc.semaphore("rows_out"))
        block = ctx.enter_context(nc.Block())

        @block.sync
        def _(sp):
            n = 0
            for dst, src in ((taps[:, :, :], d["taps"]), (raw[:, 0, :], d["bf"]), (raw[:, 1, :], d["bi"]),
                             (raw[:, 2, :], d["bd"]), (raw[:, 3, :], d["b_out"]),
                             (kmraw[:, :], d["km"]), (kmsign[:, :], d["km_sign"]),
                             (s["wfi"][:, 0:C], d["Wf"]), (s["wfi"][:, C:2 * C], d["Wi"]), (s["wd"][:, :], d["Wd"]),
                             (s["wout"][:, :], d["W_out"]), (s["ident"][:, :], d["ident"]),
                             (s["mask"][:, :], d["mask"]), (s["apad"][:, :, :], d["apad"])):
                sp.dma_start(dst, src).then_inc(loaded, 16)
                n += 16
            assert n == 14 * 16
            sp.wait_ge(steps, 16)
            for k in range(3):
                for r in range(2):
                    sp.dma_start(s["b_fi"][k:k + 1, r, :], parts[:, k, 0:2, :].rearrange("p a c -> p (a c)")).then_inc(placed, 16)
                for r in range(4):
                    sp.dma_start(s["b_d"][k:k + 1, r, :], parts[:, k, 2, :]).then_inc(placed, 16)
                    sp.dma_start(s["b_o"][k:k + 1, r, :], parts[:, k, 3, :]).then_inc(placed, 16)
            sp.dma_start(rows_dram, rows[:, :, :].rearrange("c q n -> c (q n)")).then_inc(rows_out, 16)
            sp.wait_ge(placed, 3 * 10 * 16)
            sp.wait_ge(rows_out, 16)

        @block.vector
        def _(v):
            n = [0]

            def step(ins):
                ins.then_inc(steps, 1)
                n[0] += 1
                v.wait_ge(steps, n[0])

            step(v.memset(s["ones_n"][:, :], 1.0 / (2 * P)))
            step(v.memset(s["ones3"][:, :], 1.0))
            step(v.memset(s["tiny"][:, :], TINY))
            step(v.memset(rows[:, :, :], 0.0))
            v.wait_ge(loaded, 14 * 16)
            step(v.tensor_copy(rows[:, :, 124:131], taps[:, :, :]))
            step(v.tensor_copy(rows[:, :, 0:3], taps[:, :, 4:7]))
            step(v.tensor_copy(rows[:, :, 252:255], taps[:, :, 0:3]))
            step(v.tensor_scalar(raw[:, 0, :], raw[:, 0, :], 2.0, None, ALU.add))
            step(v.tensor_copy(parts[:, 0, :, :], raw[:, :, :]))
            step(v.tensor_tensor(rest[:, :, :], raw[:, :, :], parts[:, 0, :, :], ALU.subtract))
            step(v.tensor_copy(parts[:, 1, :, :], rest[:, :, :]))
            step(v.tensor_tensor(raw[:, :, :], rest[:, :, :], parts[:, 1, :, :], ALU.subtract))
            step(v.tensor_copy(parts[:, 2, :, :], raw[:, :, :]))
            step(v.tensor_tensor(s["km"][:, :], kmraw[:, :], kmsign[:, :], ALU.mult))
            step(v.tensor_scalar(s["nident"][:, :], s["ident"][:, :], -1.0, None, ALU.mult))
            step(v.memset(s["half"][:, :], 0.5))


V_STEPS = ("m1 m2 fs p t d sp e g t2 b2 a1 v t4 s ep q er g1 y negx nry rx sy snx syd syt u "
           "alpha beta av w n1 n2").split()
V = {n: i + 1 for i, n in enumerate(V_STEPS)}
KV = len(V_STEPS)
A_STEPS = "ev0 ev1 fi0 fi1 sd ln tt d2 t2t2 d4 sq4".split()
A = {n: i + 1 for i, n in enumerate(A_STEPS)}
KA = len(A_STEPS)
NSUB = 2 * SUBS


def layer0(nc, x, x1, basis, s):
    with ExitStack() as ctx:
        def sb(name, shape, dt=F32):
            return ctx.enter_context(nc.sbuf_tensor(name, shape, dt))

        def sem(name):
            return ctx.enter_context(nc.semaphore(name))

        xt = [sb(f"xt{i}", [P, WB, C]) for i in range(2)]
        ot = sb("ot", [P, C, WB])
        tab = {n: sb(f"tab_{n}", [P, WB * CH]) for n in ("Ar", "Ai", "A2", "Br", "Bi")}
        xnT = [sb(f"xnT{i}", [P, SW, P]) for i in range(2)]
        fi = [sb(f"fi{i}", [P, SW, 2 * C]) for i in range(2)]
        ld = [sb(f"ld{i}", [P, FULL]) for i in range(2)]
        NT = 21
        tmp = sb("tmp", [P, NT, HALF])
        ebuf = tmp[0:2 * TAPS * TAPS, 12:20, :].rearrange("p a n -> p (a n)").rearrange("p (w h) -> p w h", h=P)
        m1, m2, n1, n2, sp_, vv, av, fm = (sb(n, [P, FULL]) for n in ("m1", "m2", "n1", "n2", "spg", "vv", "av", "fm"))
        scale, shift = ([sb(f"{n}{i}", [C, 1]) for i in range(2)] for n in ("scale", "shift"))
        pT = ctx.enter_context(nc.psum_tensor("pT", [P, 2, 512], F32))
        pZ = ctx.enter_context(nc.psum_tensor("pZ", [P, 4, 512], F32))
        pD = ctx.enter_context(nc.psum_tensor("pD", [P, 2, 512], F32))
        x_in, x1_out, e_in = [sem(f"x_in{i}") for i in range(2)], sem("x1_out"), sem("e_in")
        pe_xT, pe_z, pe_xn, pe_bx, pe_m, pe_fin = (sem(n) for n in ("pe_xT", "pe_z", "pe_xn", "pe_bx", "pe_m", "pe_fin"))
        v_done, a_done, fm_done, out_done = sem("v_done"), sem("a_done"), sem("fm_done"), sem("out_done")
        scale_set = sem("scale_set")
        tab_pe, tab_v, tab_a = sem("tab_pe"), sem("tab_v"), sem("tab_a")
        block = ctx.enter_context(nc.Block())

        (t, d, tt, d2, e, t2, t2t2, t4, d4, sq4, b2, a1, ss, q, er, ep, g1, y, negx, nry, rx) = (
            tmp[:, i, :] for i in range(NT))

        def vn(sblk, name, back=0):
            return sblk * KV + ((2 - back) * KV + V[name])

        def an(sblk, name, back=0):
            return sblk * KA + ((2 - back) * KA + A[name])

        def xnn(sblk, j, back=0):
            return sblk * 2 + (4 - 2 * back + j + 1)

        def tail_n(sblk, back=0):
            return sblk + (3 - back)

        TV = 27
        TA = 2
        NIT = B * SUBS // NSUB

        def walk(eng, tables, front, middle, tail):
            with eng.Fori(0, NWB) as wb:
                def number(ip, k):
                    return wb * (B * SUBS) + (ip * NSUB + k)

                def body(ip, last):
                    for k in range(NSUB):
                        first = isinstance(ip, int) and ip == 0 and k == 0
                        middle(wb, number(ip, k), k, None if first else number(ip, k - 1), (k - 1) % NSUB)
                        if k < NSUB - 1:
                            front(wb, ip * 2 + (k + 1) // SUBS, wb * (B // 2) + ip, number(ip, k + 1), k + 1)
                        elif not last:
                            front(wb, ip * 2 + 2, wb * (B // 2) + ip + 1, number(ip, k + 1), 0)

                tables(wb)
                front(wb, 0, wb * (B // 2), number(0, 0), 0)
                body(0, False)
                with eng.Fori(1, NIT - 1) as ip:
                    body(ip, False)
                body(NIT - 1, True)
                tail(number(NIT - 1, NSUB - 1), NSUB - 1)

        @block.sync
        def _(sp):
            sp.sem_inc(x1_out, 16)
            with sp.Fori(0, NWB) as wb:
                def load(b, u):
                    sp.dma_start(xt[u][:, :, :].rearrange("p w c -> p (w c)"),
                                 x[bass.ds(b, 1), :, bass.ds(wb * WB, WB), :].rearrange("a h w c -> (a h) (w c)")
                                 ).then_inc(x_in[u], 16)

                def store(b):
                    sp.wait_ge(out_done, tail_n((wb * B + b) * SUBS + SUBS - 1))
                    dst = x1[:, :, bass.ds(b, 1), bass.ds(wb, 1), :, :].rearrange("g h a e c w -> h g (a e c w)")
                    sp.dma_start(dst, ot[:, :, :].rearrange("p (g c) w -> p g (c w)", g=G)).then_inc(x1_out, 16)

                sp.wait_ge(tab_pe, wb * 4 + 1)
                sp.dma_start(ebuf, basis[:, bass.ds(wb * WB, WB), :]).then_inc(e_in, 16)
                for u in range(2):
                    load(u, u)
                with sp.Fori(0, B // 2 - 1) as ip:
                    for u in range(2):
                        store(ip * 2 + u)
                        load(ip * 2 + (2 + u), u)
                for u in range(2):
                    store(B - 2 + u)
            sp.wait_ge(x1_out, 16 * (TILES + 1))

        @block.tensor
        def _(pe):
            pe.sem_inc(pe_xn, 4)
            pe.sem_inc(pe_fin, 2)
            pe.sem_inc(pe_m, 2)
            pe.sem_inc(tab_pe, 1)

            def tables(wb):
                pe.wait_ge(e_in, (wb + 1) * 16)
                pe.wait_ge(out_done, tail_n(wb * (B * SUBS), back=1))
                for j in range(4):
                    pe.wait_ge(tab_v, wb * TV + (4 * j + 1))
                    for w in range(SW):
                        last = pe.matmul(pZ[:, w // 2, (w % 2) * 256:(w % 2) * 256 + 256],
                                         ebuf[:, j * SW + w, :], s["km"][:, :], start=True, stop=True)
                    last.then_inc(tab_pe, 1)
                pe.wait_ge(tab_v, wb * TV + (16 + 1))

            def front(wb, b, pair, sblk, k):
                par, u, kt = k % 2, k // SUBS, k % SUBS
                if kt == 0:
                    pe.wait_ge(x_in[u], (pair + 1) * 16)
                pe.wait_ge(v_done, vn(sblk, "v", back=1))
                for j in range(2):
                    for w in range(4):
                        last = pe.transpose(pT[:, j, w * P:(w + 1) * P], xt[u][:, kt * SW + 4 * j + w, :], s["ident"][:, :])
                    last.then_inc(pe_xT, 1)
                pe.wait_ge(fm_done, tail_n(sblk, back=2))
                pe.wait_ge(out_done, tail_n(sblk, back=2))
                for j in range(2):
                    pe.wait_ge(a_done, an(sblk, f"ev{j}"))
                    for bank in (2 * j, 2 * j + 1):
                        pe.matmul(pZ[:, bank, :], s["ones3"][0:3, :], s["b_fi"][0:3, :, :], start=True, stop=False)
                        for w in (2 * bank, 2 * bank + 1):
                            last = pe.matmul(pZ[:, bank, (w % 2) * 256:(w % 2) * 256 + 256], xnT[par][:, w, :],
                                             s["wfi"][:, :], start=False, stop=w % 2 == 1)
                    last.then_inc(pe_z, 1)
                pe.wait_ge(v_done, vn(sblk, "sp", back=1))
                for bank in range(2):
                    pe.matmul(pD[:, bank, :], s["ones3"][0:3, :], s["b_d"][0:3, :, :], start=True, stop=False)
                    for w in range(4):
                        last = pe.matmul(pD[:, bank, w * C:(w + 1) * C], xnT[par][:, 4 * bank + w, :],
                                         s["wd"][:, :], start=False, stop=w == 3)
                last.then_inc(pe_z, 1)
                for j in range(2):
                    for w in range(4):
                        last = pe.transpose(pT[:, j, w * P:(w + 1) * P], xnT[par][:, 4 * j + w, :], s["ident"][:, :])
                    last.then_inc(pe_xn, 1)

            def part(ap, i):
                return view(ap[:, i * CH:i * CH + 1], [C, SW], [1, CH])

            def complex_sum(ps, a, b):
                pe.matmul(ps[:, 0, :], s["ident"][:, :], part(a, 0), start=True, stop=False)
                pe.matmul(ps[:, 0, :], s["nident"][:, :], part(b, 1), start=False, stop=True)
                pe.matmul(ps[:, 1, :], s["ident"][:, :], part(a, 1), start=True, stop=False)
                return pe.matmul(ps[:, 1, :], s["ident"][:, :], part(b, 0), start=False, stop=True)

            def m_sum(sblk):
                pe.wait_ge(v_done, vn(sblk, "n2"))
                complex_sum(pZ, n1, n2).then_inc(pe_m, 1)

            def add_up(k, srcs, start, stop):
                u, kt = k // SUBS, k % SUBS
                for j in range(2):
                    for src in srcs:
                        rhs = (xt[u][:, kt * SW + 4 * j:kt * SW + 4 * j + 4, :].rearrange("p w c -> p (w c)") if src is xt
                               else src[:, j * 512:(j + 1) * 512])
                        last = pe.matmul(pZ[:, 2 + j, :], s["ident"][:, :], rhs, start=start and src is srcs[0],
                                         stop=stop and src is srcs[-1])
                return last

            def middle(wb, sblk, k, before, kb):
                pe.wait_ge(a_done, an(sblk, "fi1"))
                if before is not None:
                    m_sum(before)
                pe.wait_ge(v_done, vn(sblk, "m2"))
                complex_sum(pT, m1, m2).then_inc(pe_bx, 1)
                if before is not None:
                    add_up(kb, (av, xt), True, False)
                    pe.wait_ge(fm_done, tail_n(before))
                    add_up(kb, (fm,), False, True).then_inc(pe_fin, 1)

            def tail(sblk, k):
                m_sum(sblk)
                pe.wait_ge(out_done, tail_n(sblk, back=1))
                add_up(k, (av, xt), True, False)
                pe.wait_ge(fm_done, tail_n(sblk))
                add_up(k, (fm,), False, True).then_inc(pe_fin, 1)

            walk(pe, tables, front, middle, tail)

        @block.scalar
        def _(act):
            act.sem_inc(a_done, 2 * KA)
            act.sem_inc(out_done, 2)

            def tables(wb):
                act.wait_ge(tab_v, wb * TV + (1 + 19))
                mag = tmp[:, 0:4, :].rearrange("p a n -> p (a n)")
                sg = tmp[:, 4:8, :].rearrange("p a n -> p (a n)")
                act.activation(mag, tab["A2"][:, :], ACT.Sqrt).then_inc(tab_a, 1)
                act.wait_ge(tab_a, wb * TA + 1)
                act.activation(sg, mag, ACT.Sigmoid).then_inc(tab_a, 1)

            def front(wb, b, pair, sblk, k):
                par, u, kt = k % 2, k // SUBS, k % SUBS
                if kt == 0:
                    for src, dst in ((s["rstd"], scale), (s["nmr"], shift)):
                        act.activation(dst[u][:, :], src[:, bass.ds(b, 1)], ACT.Copy).then_inc(scale_set, 1)
                    act.wait_ge(scale_set, (pair * 2 + u) * 2 + 2)
                for j in range(2):
                    act.wait_ge(pe_xT, sblk * 2 + (j + 1))
                    act.wait_ge(pe_xn, xnn(sblk, 1, back=2))
                    act.activation(xnT[par][:, 4 * j:4 * j + 4, :].rearrange("p a n -> p (a n)"), pT[:, j, :], ACT.Identity,
                                   bias=shift[u][:, :], scale=scale[u][:, :]).then_inc(a_done, 1)
                act.wait_ge(fm_done, tail_n(sblk, back=2))
                for j in range(2):
                    act.wait_ge(pe_z, sblk * 3 + (j + 1))
                    act.activation(fi[par][:, 4 * j:4 * j + 4, :].rearrange("p a n -> p (a n)"),
                                   pZ[:, 2 * j:2 * j + 2, :].rearrange("p a n -> p (a n)"), ACT.Sigmoid).then_inc(a_done, 1)
                act.wait_ge(pe_z, sblk * 3 + 3)
                act.activation(ld[par][:, :], pD[:, :, :].rearrange("p a n -> p (a n)"), ACT.Sigmoid, scale=-1.0).then_inc(a_done, 1)
                act.wait_ge(a_done, an(sblk, "sd"))
                act.activation(ld[par][:, :], ld[par][:, :], ACT.Ln, bias=s["tiny"][:, :]).then_inc(a_done, 1)

            def take(sblk, k):
                kt = k % SUBS
                act.wait_ge(pe_fin, tail_n(sblk))
                if kt == 0:
                    act.wait_ge(x1_out, sblk * (16 // SUBS) + 16)
                act.activation(view(ot[:, 0, kt * SW:kt * SW + 1], [1, SW], [WB, C]),
                               pZ[:, 2:4, :].rearrange("p a (w c) -> p (a w) c", c=C), ACT.Copy).then_inc(out_done, 1)

            def middle(wb, sblk, k, before, kb):
                for name, src, dst in (("t", t, tt), ("d", d, d2), ("t2", t2, t2t2), (None, d2, d4)):
                    if name:
                        act.wait_ge(v_done, vn(sblk, name))
                    else:
                        act.wait_ge(a_done, an(sblk, "d2"))
                    act.activation(dst, src, ACT.Square).then_inc(a_done, 1)
                act.wait_ge(v_done, vn(sblk, "t4"))
                act.activation(sq4, t4, ACT.Square, bias=s["half"][:, :]).then_inc(a_done, 1)
                if before is not None:
                    take(before, kb)

            walk(act, tables, front, middle, take)

        @block.vector
        def _(v):
            v.sem_inc(v_done, 2 * KV)
            v.sem_inc(fm_done, 2)
            v.sem_inc(tab_v, 1)
            tts, tsc = v.tensor_tensor, v.scalar_tensor_tensor

            def tables(wb):
                count = [0]

                def step(ins, wait=True):
                    ins.then_inc(tab_v, 1)
                    count[0] += 1
                    if wait:
                        v.wait_ge(tab_v, wb * TV + (1 + count[0]))

                mag, sg, rc = (tmp[:, 4 * i:4 * i + 4, :].rearrange("p a n -> p (a n)") for i in range(3))
                Ar, Ai, A2 = tab["Ar"][:, :], tab["Ai"][:, :], tab["A2"][:, :]
                v.wait_ge(v_done, vn(wb * (B * SUBS), "n2", back=1))
                for j in range(4):
                    v.wait_ge(tab_pe, wb * 4 + (2 + j))
                    for i, name in enumerate(("Ar", "Ai", "Br", "Bi")):
                        step(v.tensor_scalar(tab[name][:, j * HALF:(j + 1) * HALF].rearrange("p (w c) -> p w c", c=CH),
                                             view(pZ[:, 0, i * CH:i * CH + 1], [256, SW], [1, CH]),
                                             1.0 if i < 2 else 0.1, None, ALU.mult), wait=i == 3)
                step(tts(rc, Ai, Ai, ALU.mult), wait=False)
                step(tts(A2, Ar, Ar, ALU.mult))
                step(tsc(A2, A2, 1e-8, rc, ALU.add, ALU.add))
                v.wait_ge(tab_a, wb * TA + 2)
                step(v.tensor_scalar(mag, mag, 1e-8, None, ALU.add))
                step(v.reciprocal(rc, mag))
                step(tsc(rc, sg, 0.95, rc, ALU.mult, ALU.mult))
                step(tts(Ar, Ar, rc, ALU.mult), wait=False)
                step(tts(Ai, Ai, rc, ALU.mult))
                step(tts(rc, Ai, Ai, ALU.mult), wait=False)
                step(tts(A2, Ar, Ar, ALU.mult))
                step(tts(A2, A2, rc, ALU.add), wait=False)
                assert count[0] == TV

            def pair(ap):
                return view(ap, [CH, SW], [0, 2], [1, CH])

            def w2c(ap):
                return view(ap, [C, SW], [CH, 2], [1, CH])

            def banks(ps):
                return view(ps[:, 0, 0:1], [CH, SW], [512, 2], [1, CH])

            def wc(ap):
                return ap.rearrange("p (w c) -> p w c", c=C)

            def apply_f(sblk, k):
                v.wait_ge(pe_m, tail_n(sblk))
                v.wait_ge(pe_fin, tail_n(sblk, back=1))
                tts(w2c(fm[:, :]), view(fi[k % 2][:, 0, 0:1], [2 * C, SW], [CH, 2], [1, CH]), banks(pZ), ALU.mult).then_inc(fm_done, 1)

            def front(*_):
                pass

            def middle(wb, sblk, k, before, kb):
                par, u, kt = k % 2, k // SUBS, k % SUBS
                last = [0]

                def step(name, ins_fn, follows=False):
                    assert V_STEPS[last[0]] == name, name
                    v.wait_ge(v_done, sblk * KV + (2 * KV + last[0] - (0 if follows else 1)))
                    ins_fn().then_inc(v_done, 1)
                    last[0] += 1

                cols = slice(kt * HALF, (kt + 1) * HALF)
                Ar, Ai, A2, Br, Bi = (tab[n][:, cols] for n in ("Ar", "Ai", "A2", "Br", "Bi"))
                i_full = fi[par][:, :, C:2 * C]
                fr, fim = fi[par][:, :, 0:CH], fi[par][:, :, CH:C]
                xn = pT[:, :, :].rearrange("p a n -> p (a n)")
                M1, M2, N1, N2, SP, VV, AV = (z[:, :] for z in (m1, m2, n1, n2, sp_, vv, av))
                if before is None:
                    v.wait_ge(tab_v, wb * TV + (TV + 1))
                v.wait_ge(pe_xn, xnn(sblk, 1))
                step("m1", lambda: tts(w2c(M1), w2c(xn), pair(Br), ALU.mult), True)
                step("m2", lambda: tts(w2c(M2), w2c(xn), pair(Bi), ALU.mult))
                v.wait_ge(a_done, an(sblk, "fi1"))
                step("fs", lambda: tts(b2.rearrange("p (w c) -> p w c", c=CH), fr, fim, ALU.add))
                step("p", lambda: tts(a1.rearrange("p (w c) -> p w c", c=CH), fr, fim, ALU.mult))
                step("t", lambda: tts(t, b2, Ar, ALU.mult))
                step("d", lambda: tts(d, a1, A2, ALU.mult))
                v.wait_ge(a_done, an(sblk, "ln"))
                step("sp", lambda: tsc(SP, ld[par][:, :], -1.0, pD[:, :, :].rearrange("p a n -> p (a n)"), ALU.mult, ALU.max))
                if before is not None:
                    apply_f(before, kb)
                v.wait_ge(a_done, an(sblk, "tt"))
                step("e", lambda: tts(e, tt, d, ALU.subtract))
                step("g", lambda: tts(wc(SP), wc(SP), i_full, ALU.mult))
                step("t2", lambda: tts(t2, e, d, ALU.subtract))
                step("b2", lambda: tts(b2, e, d, ALU.mult))
                step("a1", lambda: tts(a1, t2, t, ALU.mult))
                v.wait_ge(pe_bx, sblk + 1)
                step("v", lambda: tts(w2c(VV), w2c(SP), banks(pT), ALU.mult))
                v.wait_ge(a_done, an(sblk, "t2t2"))
                step("t4", lambda: tsc(t4, d2, -2.0, t2t2, ALU.mult, ALU.add))
                step("s", lambda: tsc(ss, t, 1.0, e, ALU.add, ALU.add))
                v.wait_ge(a_done, an(sblk, "d4"))
                step("ep", lambda: tsc(ep, t4, 1.0, d4, ALU.add, ALU.mult))
                v.wait_ge(a_done, an(sblk, "sq4"))
                step("q", lambda: tsc(q, sq4, 0.75, d4, ALU.add, ALU.subtract))
                step("er", lambda: tsc(er, t, 1.0, d, ALU.add, ALU.mult))
                step("g1", lambda: tts(g1, q, b2, ALU.mult))
                step("y", lambda: tts(y, q, a1, ALU.mult))
                step("negx", lambda: tsc(negx, ep, -1.0, g1, ALU.add, ALU.add))
                step("nry", lambda: tsc(nry, er, -1.0, y, ALU.add, ALU.mult))
                step("rx", lambda: tsc(rx, er, -1.0, negx, ALU.add, ALU.mult))
                step("sy", lambda: tts(ep, ss, y, ALU.mult))
                step("snx", lambda: tts(g1, ss, negx, ALU.mult))
                step("syd", lambda: tts(t2, ep, d, ALU.mult))
                step("syt", lambda: tts(t2t2, ep, t, ALU.mult))
                step("u", lambda: tts(nry, nry, g1, ALU.add))
                step("alpha", lambda: tts(rx, rx, t2, ALU.subtract))
                step("beta", lambda: tts(t2t2, t2t2, nry, ALU.subtract))
                v.wait_ge(pe_fin, tail_n(sblk, back=1))
                step("av", lambda: tts(w2c(AV), pair(rx), w2c(VV), ALU.mult))
                step("w", lambda: tts(w2c(SP), pair(t2t2), w2c(VV), ALU.mult))
                step("n1", lambda: tts(w2c(N1), w2c(SP), pair(Ar), ALU.mult), True)
                step("n2", lambda: tts(w2c(N2), w2c(SP), pair(Ai), ALU.mult))
                assert last[0] == KV

            walk(v, tables, front, middle, apply_f)


def channel_steps(last):
    dve, act = [], []
    for cc in range(CG):
        prep = not (last and cc == CG - 1)
        if not last and cc == 3:
            dve += ["mean", "de", "do", "m2", "dq", "ds", "vs", "ve", "rs"]
            act += ["sq"]
        if prep:
            dve += [f"{n}{cc}" for n in ("xs", "xm", "hl", "hr", "xl", "tl")]
            act += [f"{n}{cc}" for n in ("xh", "th")]
        act += [f"{n}{cc}" for n in ("z0_", "z1_", "z2_", "z3_", "ga")]
        if not last and cc == 2:
            dve += [f"bn{b}" for b in range(B)]
        dve += [f"{n}{cc}" for n in ("at", "c2_", "c4_", "f0_", "f1_", "f2_", "bt0_", "bt1_", "bt2_", "bt3_", "sp", "o", "oa", "ob")]
        act += [f"{n}{cc}" for n in ("s1_", "c1_", "sb", "ln")]
    return dve, act


def layer1_conv(nc, x1, hs, rows_dram, s):
    XW = W + 10
    with ExitStack() as ctx:
        def sb(name, shape, dt=F32):
            return ctx.enter_context(nc.sbuf_tensor(name, shape, dt))

        def sem(name):
            return ctx.enter_context(nc.semaphore(name))

        NQ = 3 * TAPS
        xg = sb("xg", [P, B, NWB, CG, WB])
        traw = [sb(f"traw{i}", [P, NQ, P]) for i in range(2)]
        thi = [sb(f"thi{i}", [P, 2 * TAPS, P], F32R) for i in range(2)]
        tlo = [sb(f"tlo{i}", [P, 2 * TAPS, P], F32R) for i in range(2)]
        xn = [sb(f"xn{i}", [P, B, XW]) for i in range(2)]
        xhi = [sb(f"xhi{i}", [P, B, XW], F32R) for i in range(2)]
        xlo = [sb(f"xlo{i}", [P, B, XW], F32R) for i in range(2)]
        og = sb("og", [P, B, NWB, CG, WB])
        gate = sb("gate", [P, B * W])
        bt = sb("bt", [P, B * W])
        lns = sb("lns", [P, B * W])
        st = sb("st1", [P, B, 6])
        mean = sb("mean1", [P, B])
        rstd = sb("rstd1", [P, B])
        dev = sb("dev1", [P, 2, B])
        vs = sb("vs1", [P, B])
        ve = sb("ve1", [P, B])
        sq = sb("sq1", [P, B])
        sga, at, s1, c1, c2, c4, ff = (sb(n, [P, B, 8]) for n in ("sga", "at", "s1", "c1", "c2", "c4", "ff"))
        pG = ctx.enter_context(nc.psum_tensor("pG", [P, 4, 512], F32))
        pB = ctx.enter_context(nc.psum_tensor("pB", [P, 4, 512], F32))
        pe_zg, pe_zb, pe_ga, pe_mean, pe_var = (sem(n) for n in ("pe_zg", "pe_zb", "pe_ga", "pe_mean", "pe_var"))
        v_done, a_done = sem("cv_done"), sem("ca_done")
        xg_in, t_in = sem("xg_in"), [sem(f"t_in{i}") for i in range(2)]
        hs_out = sem("hs_out")
        first_v, first_a, first_p = sem("first_v"), sem("first_a"), sem("first_p")
        block = ctx.enter_context(nc.Block())

        names = {last: channel_steps(last) for last in (False, True)}
        place = {last: [{n: i + 1 for i, n in enumerate(x)} for x in names[last]] for last in (False, True)}
        KV1, KA1 = (len(x) for x in names[False])

        def vc(g, name, last=False, back=0):
            return g * KV1 + ((1 - back) * KV1 + place[last][0][name])

        def ac(g, name, last=False, back=0):
            return g * KA1 + ((1 - back) * KA1 + place[last][1][name])

        def chan(g, cc):
            return g * CG + (cc + 2)

        def groups(eng, do):
            with eng.Fori(0, G // 2 - 1) as i:
                for gp in range(2):
                    do(i * 2 + gp, False)
            do(G - 2, False)
            do(G - 1, True)

        @block.sync
        def _(sp):
            sp.sem_inc(hs_out, 16)

            def load_group(g):
                src = x1[g] if isinstance(g, int) else x1[bass.ds(g, 1)].rearrange("a h b e c w -> (a h) b e c w")
                sp.dma_start(xg[:, :, :, :, :].rearrange("p b e c w -> p (b e c w)"),
                             src.rearrange("h b e c w -> h (b e c w)")).then_inc(xg_in, 16)

            def load_taps(c, par):
                base = rows_dram[bass.ds(c, 1), :]
                src = bass.AP(base.tensor, base.offset, [[1, P], [256, NQ], [1, P]])
                sp.dma_start(traw[par][:, :, :], src).then_inc(t_in[par], 16)

            load_group(0)
            for i in range(2):
                load_taps(i, i)

            def do(g, last):
                for cc in range(CG):
                    if cc == 2 and not last:
                        sp.wait_ge(v_done, vc(g, "hr2"))
                        load_group(g + 1)
                    if not (last and cc >= 2):
                        sp.wait_ge(pe_ga, chan(g, cc) + 1)
                        load_taps(g * CG + (cc + 2), cc % 2)
                sp.wait_ge(v_done, vc(g, "ob3", last))
                dst = (hs[g] if isinstance(g, int) else hs[bass.ds(g, 1)].rearrange("a h b e c w -> (a h) b e c w"))
                sp.dma_start(dst.rearrange("h b e c w -> h (b e c w)"),
                             og[:, :, :, :, :].rearrange("p b e c w -> p (b e c w)")).then_inc(hs_out, 16)

            groups(sp, do)
            sp.wait_ge(hs_out, 16 * (G + 1))

        @block.tensor
        def _(pe):
            pe.sem_inc(pe_zg, 8)
            pe.sem_inc(pe_zb, 8)
            pe.sem_inc(pe_ga, 2)
            pe.sem_inc(pe_mean, 1)
            pe.sem_inc(pe_var, 1)

            def mean_mm():
                pe.matmul(pB[:, 0, 0:B], s["ones_n"][:, :], st[:, :, 1], start=True, stop=False)
                return pe.matmul(pB[:, 0, 0:B], s["ones_n"][:, :], st[:, :, 4], start=False, stop=True)

            def var_mm():
                return pe.matmul(pB[:, 0, 0:B], s["ones_n"][:, :], vs[:, :], start=True, stop=True)

            pe.wait_ge(first_v, B)
            mean_mm().then_inc(first_p, 1)
            pe.wait_ge(first_v, B + 7)
            var_mm().then_inc(first_p, 1)

            def conv(ps, q0, par, taps):
                last = []
                for j in taps:
                    for t, xs in ((thi, xhi), (thi, xlo), (tlo, xhi)):
                        for k in range(4):
                            fin = j == TAPS - 1 and t is tlo
                            m = pe.matmul(ps[:, k, :], t[par][:, q0 + j, :],
                                          xs[par][:, 4 * k:4 * k + 4, 10 - j:10 - j + W],
                                          start=j == 0 and xs is xhi and t is thi, stop=fin)
                            if fin:
                                last.append(m)
                return last

            def do(g, last):
                for cc in range(CG):
                    par = cc % 2
                    if cc == 0:
                        pe.wait_ge(v_done, vc(g, "tl3", back=1))
                        pe.wait_ge(a_done, ac(g, "ga3", back=1))
                    else:
                        pe.wait_ge(v_done, vc(g, f"tl{cc - 1}", last))
                        pe.wait_ge(a_done, ac(g, f"ga{cc - 1}", last))
                    conv(pG, 0, par, range(3))
                    if cc == 3 and not last:
                        pe.wait_ge(v_done, vc(g, "bt3_2"))
                        mean_mm().then_inc(pe_mean, 1)
                    conv(pG, 0, par, range(3, 5))
                    if cc == 3 and not last:
                        pe.wait_ge(v_done, vc(g, "vs"))
                        var_mm().then_inc(pe_var, 1)
                    for m in conv(pG, 0, par, range(5, TAPS)):
                        m.then_inc(pe_zg, 1)
                    if cc == 3 and not last:
                        pe.wait_ge(v_done, vc(g, "ve"))
                    pe.wait_ge(v_done, vc(g, "bt3_3", back=1) if cc == 0 else vc(g, f"bt3_{cc - 1}", last))
                    conv(pB, TAPS, par, range(3))
                    pe.wait_ge(a_done, ac(g, f"z0_{cc}", last))
                    for j in range(TAPS):
                        m = pe.matmul(pG[:, 0, 0:B * 8], traw[par][:, 2 * TAPS + j, :],
                                      xn[par][:, :, 6 - j:6 - j + 8], start=j == 0, stop=j == TAPS - 1)
                    m.then_inc(pe_ga, 1)
                    for m in conv(pB, TAPS, par, range(3, TAPS)):
                        m.then_inc(pe_zb, 1)

            groups(pe, do)

        @block.scalar
        def _(act):
            def split(par, tick):
                tick("xh", lambda: act.activation(xhi[par][:, :, :].rearrange("p b w -> p (b w)"),
                                                  xn[par][:, :, :].rearrange("p b w -> p (b w)"), ACT.Copy))
                tick("th", lambda: act.activation(thi[par][:, :, :].rearrange("p q m -> p (q m)"),
                                                  traw[par][:, 0:2 * TAPS, :].rearrange("p q m -> p (q m)"), ACT.Copy))

            act.wait_ge(first_v, B + 8)
            act.activation(sq[:, :], ve[:, :], ACT.Sqrt).then_inc(first_a, 1)
            act.wait_ge(first_v, B + 13)
            act.wait_ge(t_in[0], 16)
            split(0, lambda name, f: f().then_inc(first_a, 1))
            act.sem_inc(a_done, KA1)

            def do(g, last):
                for cc in range(CG):
                    nxt = (cc + 1) % 2

                    def step(name, f):
                        f().then_inc(a_done, 1)

                    if cc == 3 and not last:
                        act.wait_ge(v_done, vc(g, "ve"))
                        step("sq", lambda: act.activation(sq[:, :], ve[:, :], ACT.Sqrt))
                    if not (last and cc == CG - 1):
                        act.wait_ge(v_done, vc(g, f"hr{cc}", last))
                        act.wait_ge(pe_zb, chan(g, cc) * 4)
                        act.wait_ge(t_in[nxt], (g * 2 + (1 + (cc + 1) // 2)) * 16)
                        split(nxt, step)
                    for k in range(4):
                        act.wait_ge(pe_zg, chan(g, cc) * 4 + (k + 1))
                        if k == 0:
                            act.wait_ge(v_done, vc(g, "bt3_3", back=1) if cc == 0 else vc(g, f"bt3_{cc - 1}", last))
                        step("z", lambda: act.activation(gate[:, k * 512:(k + 1) * 512], pG[:, k, :], ACT.Sigmoid))
                    act.wait_ge(pe_ga, chan(g, cc) + 1)
                    step("ga", lambda: act.activation(sga[:, :, :].rearrange("p b w -> p (b w)"), pG[:, 0, 0:B * 8], ACT.Sigmoid))
                    act.wait_ge(v_done, vc(g, f"at{cc}", last))
                    step("s1", lambda: act.activation(s1[:, :, :], at[:, :, :], ACT.Sigmoid))
                    step("c1", lambda: act.activation(c1[:, :, :], at[:, :, :], ACT.Sigmoid, scale=-1.0))
                    act.wait_ge(v_done, vc(g, f"bt3_{cc}", last))
                    step("sb", lambda: act.activation(lns[:, :], bt[:, :], ACT.Sigmoid, scale=-1.0))
                    act.wait_ge(a_done, ac(g, f"sb{cc}", last))
                    step("ln", lambda: act.activation(lns[:, :], lns[:, :], ACT.Ln, bias=s["tiny"][:, :]))

            groups(act, do)

        @block.vector
        def _(v):
            tts, tsc = v.tensor_tensor, v.scalar_tensor_tensor

            def bn(b):
                return v.bn_stats(st[:, b, :], xg[:, b, :, :, :].rearrange("p e c w -> p (e c w)"))

            def stats_mid():
                yield "mean", lambda: v.tensor_copy(mean[:, :], pB[:, 0, 0:B])
                yield "de", lambda: tts(dev[:, 0, :], st[:, :, 1], pB[:, 0, 0:B], ALU.subtract)
                yield "do", lambda: tts(dev[:, 1, :], st[:, :, 4], pB[:, 0, 0:B], ALU.subtract)
                yield "m2", lambda: tts(vs[:, :], st[:, :, 2], st[:, :, 5], ALU.add)
                yield "dq", lambda: tts(dev[:, :, :], dev[:, :, :], dev[:, :, :], ALU.mult)
                yield "ds", lambda: tts(dev[:, 0, :], dev[:, 0, :], dev[:, 1, :], ALU.add)
                yield "vs", lambda: tsc(vs[:, :], vs[:, :], 1.0 / (W * CG // 2), dev[:, 0, :], ALU.mult, ALU.add)

            def ve_():
                return v.tensor_scalar(ve[:, :], pB[:, 0, 0:B], GN_EPS, None, ALU.add)

            def rs_():
                return v.reciprocal(rstd[:, :], sq[:, :])

            def norm(cc, par, step):
                src = view(xg[:, 0, 0, cc, 0:1], [NWB * CG * WB, B], [CG * WB, NWB], [1, WB])
                mid = view(xn[par][:, 0, 7:8], [XW, B], [WB, NWB], [1, WB])
                step("xs", lambda: tts(mid, src, view(mean[:, 0:1], [1, B], [0, NWB], [0, WB]), ALU.subtract))
                step("xm", lambda: tts(xn[par][:, :, 7:7 + W], xn[par][:, :, 7:7 + W],
                                       view(rstd[:, 0:1], [1, B], [0, W]), ALU.mult))
                step("hl", lambda: v.tensor_copy(xn[par][:, :, 0:7], xn[par][:, :, W:W + 7]))
                step("hr", lambda: v.tensor_copy(xn[par][:, :, W + 7:W + 10], xn[par][:, :, 7:10]))

            def low(par, step):
                step("xl", lambda: tts(xlo[par][:, :, :], xn[par][:, :, :], xhi[par][:, :, :].bitcast(F32), ALU.subtract))
                step("tl", lambda: tts(tlo[par][:, :, :], traw[par][:, 0:2 * TAPS, :], thi[par][:, :, :].bitcast(F32), ALU.subtract))

            n = [0]

            def first(name, f):
                f().then_inc(first_v, 1)
                n[0] += 1
                v.wait_ge(first_v, n[0])

            v.wait_ge(xg_in, 16)
            for b in range(B):
                first("bn", lambda: bn(b))
            v.wait_ge(first_p, 1)
            for name, f in stats_mid():
                first(name, f)
            v.wait_ge(first_p, 2)
            first("ve", ve_)
            v.wait_ge(first_a, 1)
            first("rs", rs_)
            norm(0, 0, first)
            v.wait_ge(first_a, 3)
            low(0, first)
            assert n[0] == B + 15
            v.sem_inc(v_done, KV1)

            def do(g, last):
                done = [0]
                order = names[last][0]

                def step(name, f, follows=True):
                    assert order[done[0]] == name, (order[done[0]], name)
                    v.wait_ge(v_done, g * KV1 + (KV1 + done[0] - (0 if follows else 1)))
                    f().then_inc(v_done, 1)
                    done[0] += 1

                for cc in range(CG):
                    par, nxt = cc % 2, (cc + 1) % 2
                    if cc == 3 and not last:
                        v.wait_ge(pe_mean, g + 2)
                        for name, f in stats_mid():
                            step(name, f)
                        v.wait_ge(pe_var, g + 2)
                        step("ve", ve_)
                        v.wait_ge(a_done, ac(g, "sq"))
                        step("rs", rs_)
                    if not (last and cc == CG - 1):
                        v.wait_ge(pe_ga, chan(g, cc))
                        norm((cc + 1) % CG, nxt, lambda name, f: step(f"{name}{cc}", f))
                        v.wait_ge(a_done, ac(g, f"th{cc}", last))
                        low(nxt, lambda name, f: step(f"{name}{cc}", f))
                    if cc == 2 and not last:
                        v.wait_ge(xg_in, g * 16 + 32)
                        for b in range(B):
                            step(f"bn{b}", lambda: bn(b), False)
                    c = g * CG + cc
                    v.wait_ge(a_done, ac(g, f"ga{cc}", last))
                    step(f"at{cc}", lambda: tts(at[:, :, :], sga[:, :, :], apad_of(c), ALU.mult))
                    v.wait_ge(a_done, ac(g, f"c1_{cc}", last))
                    step(f"c2_{cc}", lambda: tts(c2[:, :, :], c1[:, :, :], c1[:, :, :], ALU.mult))
                    step(f"c4_{cc}", lambda: tts(c4[:, :, :], c2[:, :, :], c2[:, :, :], ALU.mult))
                    fl = [z[:, :, :].rearrange("p b w -> p (b w)") for z in (ff, c1, c2, c4, s1)]
                    step(f"f0_{cc}", lambda: tsc(fl[0], fl[1], 1.0, fl[4], ALU.add, ALU.mult))
                    step(f"f1_{cc}", lambda: tsc(fl[0], fl[2], 1.0, fl[0], ALU.add, ALU.mult))
                    step(f"f2_{cc}", lambda: tsc(fl[0], fl[3], 1.0, fl[0], ALU.add, ALU.mult))
                    for k in range(4):
                        v.wait_ge(pe_zb, chan(g, cc) * 4 + (k + 1))
                        step(f"bt{k}_{cc}", lambda: tts(bt[:, k * 512:(k + 1) * 512], gate[:, k * 512:(k + 1) * 512], pB[:, k, :], ALU.mult), False)
                    v.wait_ge(a_done, ac(g, f"ln{cc}", last))
                    step(f"sp{cc}", lambda: tsc(bt[:, :], lns[:, :], -1.0, bt[:, :], ALU.mult, ALU.max))
                    if cc == 0:
                        v.wait_ge(hs_out, g * 16 + 16)
                    step(f"o{cc}", lambda: v.tensor_scalar(view(og[:, 0, 0, cc, 0:1], [NWB * CG * WB, B], [CG * WB, NWB], [1, WB]),
                                                           bt[:, :].rearrange("p (b e w) -> p b e w", b=B, e=NWB), 1e-6, 255.0 / 256.0, ALU.add, ALU.mult))
                    step(f"oa{cc}", lambda: tsc(og[:, :, NWB - 1, cc, WB - 4:WB], view(bt[:, W - 4:W - 3], [W, B], [1, 4]), 1e-6, ff[:, :, 0:4], ALU.add, ALU.mult))
                    step(f"ob{cc}", lambda: tsc(og[:, :, 0, cc, 0:4], view(bt[:, 0:1], [W, B], [1, 4]), 1e-6, ff[:, :, 4:8], ALU.add, ALU.mult))
                assert done[0] == len(order)

            def apad_of(c):
                a = s["apad"][:, c, :] if isinstance(c, int) else s["apad"][:, bass.ds(c, 1), :]
                return view(a, [0, B], [1, 8])

            groups(v, do)


def layer1_out(nc, x1, hs, y, s):
    with ExitStack() as ctx:
        def sb(name, shape, dt=F32):
            return ctx.enter_context(nc.sbuf_tensor(name, shape, dt))

        def sem(name):
            return ctx.enter_context(nc.semaphore(name))

        ht = [sb(f"ht{i}", [P, C, WB]) for i in range(2)]
        xt = [sb(f"x1t{i}", [P, C, WB]) for i in range(2)]
        yt = [sb(f"yt{i}", [P, WB, C]) for i in range(2)]
        hT = [sb(f"hT{i}", [P, 4, P]) for i in range(2)]
        pT = [ctx.enter_context(nc.psum_tensor(f"dT{i}", [P, 512], F32)) for i in range(2)]
        pO = [ctx.enter_context(nc.psum_tensor(f"dO{i}", [P, 512], F32)) for i in range(2)]
        NQD = WB // 4
        h_in, x_in, y_out = ([sem(f"{n}{i}") for i in range(2)] for n in ("h_in", "x1_in", "y_out"))
        pe_T, pe_O, a_done, v_done = sem("pe_T"), sem("pe_O"), sem("da_done"), sem("dv_done")
        block = ctx.enter_context(nc.Block())

        def tiles(eng, body):
            with eng.Fori(0, NWB) as wb:
                with eng.Fori(0, B // 2) as ip:
                    for u in range(2):
                        for k in range(NQD):
                            body(wb * (B // 2) + ip, (wb * B + ip * 2 + u) * NQD + k, u, k)

        @block.sync
        def _(sp):
            for u in range(2):
                sp.sem_inc(y_out[u], 16)
            with sp.Fori(0, NWB) as wb:
                def load(b, u):
                    for src, dst, sm in ((hs, ht, h_in), (x1, xt, x_in)):
                        sp.dma_start(dst[u][:, :, :].rearrange("p (g c) w -> p g (c w)", g=G),
                                     src[:, :, bass.ds(b, 1), bass.ds(wb, 1), :, :].rearrange("g h a e c w -> h g (a e c w)")
                                     ).then_inc(sm[u], 16)

                def store(b, u):
                    sp.wait_ge(v_done, (wb * B + b) * NQD + (2 + NQD))
                    sp.dma_start(y[bass.ds(b, 1), :, bass.ds(wb * WB, WB), :].rearrange("a h w c -> (a h) (w c)"),
                                 yt[u][:, :, :].rearrange("p w c -> p (w c)")).then_inc(y_out[u], 16)

                for u in range(2):
                    load(u, u)
                with sp.Fori(0, B // 2 - 1) as ip:
                    for u in range(2):
                        store(ip * 2 + u, u)
                        load(ip * 2 + (2 + u), u)
                for u in range(2):
                    store(B - 2 + u, u)
            for u in range(2):
                sp.wait_ge(y_out[u], 16 * (TILES // 2 + 1))

        @block.tensor
        def _(pe):
            pe.sem_inc(pe_O, 2)

            def body(pair, n, u, k):
                r = k % 2
                if k == 0:
                    pe.wait_ge(h_in[u], (pair + 1) * 16)
                pe.wait_ge(a_done, n + 1)
                for w in range(4):
                    last = pe.transpose(pT[r][:, w * P:(w + 1) * P], ht[u][:, :, 4 * k + w], s["ident"][:, :])
                last.then_inc(pe_T, 1)
                pe.wait_ge(v_done, n + 1)
                pe.matmul(pO[r][:, :], s["ones3"][0:3, :], s["b_o"][0:3, :, :], start=True, stop=False)
                pe.wait_ge(a_done, n + 3)
                for w in range(4):
                    last = pe.matmul(pO[r][:, w * C:(w + 1) * C], hT[r][:, w, :], s["wout"][:, :], start=False, stop=w == 3)
                last.then_inc(pe_O, 1)

            tiles(pe, body)

        @block.scalar
        def _(act):
            act.sem_inc(a_done, 2)

            def body(pair, n, u, k):
                r = k % 2
                act.wait_ge(pe_T, n + 1)
                act.wait_ge(pe_O, n + 1)
                act.activation(view(hT[r][:, 0, P - 1:P], [P, 4], [-1, P]),
                               pT[r][:, :].rearrange("p (w h) -> p w h", h=P), ACT.Copy).then_inc(a_done, 1)

            tiles(act, body)

        @block.vector
        def _(v):
            v.sem_inc(v_done, 2)

            def body(pair, n, u, k):
                r = k % 2
                if k == 0:
                    v.wait_ge(x_in[u], (pair + 1) * 16)
                    v.wait_ge(y_out[u], (pair + 1) * 16)
                v.wait_ge(pe_O, n + 3)
                v.tensor_tensor(yt[u][:, 4 * k:4 * k + 4, :], view(xt[u][:, 0, 4 * k:4 * k + 1], [1, 4], [WB, C]),
                                pO[r][:, :].rearrange("p (w c) -> p w c", c=C), ALU.add).then_inc(v_done, 1)

            tiles(v, body)


PHASES = 4


def build(nc, d, y):
    with ExitStack() as ctx:
        def sb(name, shape, dt=F32):
            return ctx.enter_context(nc.sbuf_tensor(name, shape, dt))

        s = {
            "ident": sb("ident", [P, P]), "nident": sb("nident", [P, P]), "half": sb("half", [P, 1]), "mask": sb("mask", [C, G]), "ones_n": sb("ones_n", [P, P]),
            "ones3": sb("ones3", [3, P], BF16), "tiny": sb("tiny", [P, 1]),
            "wfi": sb("wfi", [C, 2 * C]), "wd": sb("wd", [C, C]), "wout": sb("wout", [C, C]),
            "km": sb("km", [2 * TAPS * TAPS, 4 * CH]), "b_fi": sb("b_fi", [3, 2, 2 * C], BF16),
            "b_d": sb("b_d", [3, 4, C], BF16), "b_o": sb("b_o", [3, 4, C], BF16),
            "apad": sb("apad", [P, C, 8]), "rstd": sb("rstd", [C, B]), "nmr": sb("nmr", [C, B]),
        }
        rows_dram = nc.dram_tensor("rows_dram", (C, 3 * TAPS * 256), F32).ap()
        x1 = nc.dram_tensor("x1", (G, H, B, NWB, CG, WB), F32).ap()
        hs = nc.dram_tensor("hs", (G, H, B, NWB, CG, WB), F32).ap()
        setup(nc, d, s, rows_dram)
        stats_of_x(nc, d["x"], s["rstd"], s["nmr"], s["ones_n"], s["mask"])
        layer0(nc, d["x"], x1, d["basis"], s)
        layer1_conv(nc, x1, hs, rows_dram, s)
        layer1_out(nc, x1, hs, y, s)


def constants():
    i = np.arange(TAPS) + (H - TAPS) // 2
    kw, kh = np.arange(W), np.arange(H)
    ang = 2 * np.pi * ((kh[None, None, None, :] * i[:, None, None, None]
                        + kw[None, None, :, None] * i[None, :, None, None]) % H) / H
    ang = ang.reshape(TAPS * TAPS, W, H)
    basis = np.concatenate([np.cos(ang), np.sin(ang)]).astype(np.float32)
    sign = np.ones((2 * TAPS * TAPS, 4 * CH), np.float32)
    sign[TAPS * TAPS:, CH:2 * CH] = -1
    sign[TAPS * TAPS:, 3 * CH:] = -1
    mask = (np.arange(C)[:, None] // CG == np.arange(G)[None]).astype(np.float32)
    return {"basis": basis, "km_sign": sign, "ident": np.eye(P, dtype=np.float32), "mask": mask}


def kernel(**inputs):
    import concourse.bacc as bacc
    from concourse.bass_utils import run_bass_kernel_spmd

    a = {k: np.asarray(v) for k, v in inputs.items()}

    def taps_first(k):
        return np.transpose(k.reshape(k.shape[0], -1))

    ar, ai, br, bi = (taps_first(a[f"L0_conv_{n}"]) for n in ("A_real", "A_imag", "B_real", "B_imag"))
    km = np.concatenate([np.concatenate([ar, ai, br, bi], 1), np.concatenate([ai, ar, bi, br], 1)], 0)
    taps = np.stack([np.transpose(a[f"L1_conv_{n}"], (0, 2, 1))[:, :, ::-1] for n in ("gate_B_kernel", "B_kernel", "gate_A_kernel")], 1)
    apad = np.zeros((P, C, 8), np.float32)
    apad[H - 1 - (np.arange(TAPS) - TAPS // 2) % H, :, 1:] = np.transpose(a["L1_conv_A_kernel"], (1, 0, 2))
    arrays = {
        "x": a["x"], "Wf": a["L0_conv_Wf"], "Wi": a["L0_conv_Wi"], "Wd": a["L0_conv_Wd"], "W_out": a["L1_conv_W_out"],
        "bf": a["L0_conv_bf"][None], "bi": a["L0_conv_bi"][None], "bd": a["L0_conv_bd"][None], "b_out": a["L1_conv_b_out"][None],
        "km": km, "taps": taps.reshape(C, 3 * TAPS, TAPS), "apad": apad, **constants(),
    }
    arrays = {f"in_{k}": np.ascontiguousarray(v) for k, v in arrays.items()}
    nc = bacc.Bacc("TRN2", target_bir_lowering=False, num_devices=1)
    d = {k[3:]: nc.dram_tensor(k, v.shape, mybir.dt.from_np(v.dtype), kind="ExternalInput").ap() for k, v in arrays.items()}
    y = nc.dram_tensor("out_y", (B, H, W, C), F32, kind="ExternalOutput").ap()
    build(nc, d, y)
    r = run_bass_kernel_spmd(nc, [arrays], core_ids=[0])
    return r.results[0]["out_y"]
```

```python
from contextlib import ExitStack

import numpy as np
import concourse.bass as bass
from concourse import mybir

F32 = mybir.dt.float32
F32R = mybir.dt.float32r
BF16 = mybir.dt.bfloat16
ALU = mybir.AluOpType
ACT = mybir.ActivationFunctionType
AX = mybir.AxisListType

P = 128
B, H, W, C = 16, 128, 128, 128
CH = C // 2
TAPS = 7
G = 32
CG = C // G
WB = 32
NWB = W // WB
TILES = NWB * B
SW = 8
SUBS = WB // SW
HALF = SW * CH
FULL = SW * C
OH = 26
HB = -(-H // OH)
IH = OH + TAPS - 1
EDGE = TAPS // 2
HPAD = HB * OH + TAPS - 1
NQ = 3 * NWB
RW = IH + OH - 1
GN_EPS = 1e-5
TINY = 2.0 ** -63


def view(ap, *dims):
    return bass.AP(ap.tensor, ap.offset, [list(ap.ap[0])] + [list(d) for d in dims])


def stats_of_x(nc, x, rstd_c, nmr_c, ones_n, mask):
    NPX = B * G
    with ExitStack() as ctx:
        img = [ctx.enter_context(nc.sbuf_tensor(f"img{i}", [P, W * C], F32)) for i in range(2)]
        st = ctx.enter_context(nc.sbuf_tensor("xst", [P, B, G, 6], F32))
        dev = ctx.enter_context(nc.sbuf_tensor("xdev", [P, 2, NPX], F32))
        m2 = ctx.enter_context(nc.sbuf_tensor("xm2", [P, NPX], F32))
        mean = ctx.enter_context(nc.sbuf_tensor("xmean", [P, NPX], F32))
        sd = ctx.enter_context(nc.sbuf_tensor("xsd", [P, NPX], F32))
        rs = ctx.enter_context(nc.sbuf_tensor("xrs", [P, NPX], F32))
        mps = ctx.enter_context(nc.psum_tensor("xmean_ps", [P, NPX], F32))
        vps = ctx.enter_context(nc.psum_tensor("xvar_ps", [P, NPX], F32))
        img_in = [ctx.enter_context(nc.semaphore(f"img_in{i}")) for i in range(2)]
        counted = ctx.enter_context(nc.semaphore("counted"))
        mean_ready = ctx.enter_context(nc.semaphore("mean_ready"))
        var_ready = ctx.enter_context(nc.semaphore("var_ready"))
        sd_ready = ctx.enter_context(nc.semaphore("sd_ready"))
        steps = ctx.enter_context(nc.semaphore("xsteps"))
        block = ctx.enter_context(nc.Block())

        @block.sync
        def _(sp):
            for u in range(2):
                sp.dma_start(img[u][:, :], x[u].rearrange("h w c -> h (w c)")).then_inc(img_in[u], 16)
            with sp.Fori(0, B // 2 - 1) as i:
                for u in range(2):
                    sp.wait_ge(counted, (i * 2 + (u + 1)) * G)
                    src = x[bass.ds(i * 2 + (2 + u), 1)].rearrange("a h w c -> (a h) (w c)")
                    sp.dma_start(img[u][:, :], src).then_inc(img_in[u], 16)

        @block.vector
        def _(v):
            with v.Fori(0, B // 2) as i:
                for u in range(2):
                    v.wait_ge(img_in[u], (i + 1) * 16)
                    for g in range(G):
                        v.bn_stats(st[:, bass.ds(i * 2 + u, 1), g, :],
                                   view(img[u][:, g * CG:g * CG + 1], [C, W], [1, CG])).then_inc(counted, 1)
            n = [0]

            def step(ins):
                ins.then_inc(steps, 1)
                n[0] += 1
                v.wait_ge(steps, n[0])

            fl = st[:, :, :, :].rearrange("p b g s -> p (b g) s")
            v.wait_ge(mean_ready, 1)
            step(v.tensor_tensor(dev[:, 0, :], fl[:, :, 1], mps[:, :], ALU.subtract))
            step(v.tensor_tensor(dev[:, 1, :], fl[:, :, 4], mps[:, :], ALU.subtract))
            step(v.tensor_copy(mean[:, :], mps[:, :]))
            step(v.tensor_tensor(m2[:, :], fl[:, :, 2], fl[:, :, 5], ALU.add))
            step(v.tensor_tensor(dev[:, :, :], dev[:, :, :], dev[:, :, :], ALU.mult))
            step(v.tensor_tensor(dev[:, 0, :], dev[:, 0, :], dev[:, 1, :], ALU.add))
            step(v.scalar_tensor_tensor(dev[:, 0, :], m2[:, :], 1.0 / (W * CG // 2), dev[:, 0, :],
                                        ALU.mult, ALU.add))
            v.wait_ge(var_ready, 1)
            step(v.tensor_scalar(m2[:, :], vps[:, :], GN_EPS, None, ALU.add))
            v.wait_ge(sd_ready, 1)
            step(v.reciprocal(rs[:, :], sd[:, :]))
            step(v.scalar_tensor_tensor(mean[:, :], mean[:, :], -1.0, rs[:, :], ALU.mult, ALU.mult))
            for src, dst in ((rs, rstd_c), (mean, nmr_c)):
                step(v.tensor_tensor(dev[:, 0, :].rearrange("p (b g) -> p b g", g=G),
                                     src[:, :].rearrange("p (b g) -> p b g", g=G),
                                     view(mask[:, 0:1], [0, B], [1, G]), ALU.mult))
                step(v.reduce_sum(dst[:, :], dev[:, 0, :].rearrange("p (b g) -> p b g", g=G), axis=AX.X))

        @block.tensor
        def _(pe):
            fl = st[:, :, :, :].rearrange("p b g s -> p (b g) s")
            pe.wait_ge(counted, B * G)
            pe.matmul(mps[:, :], ones_n[:, :], fl[:, :, 1], start=True, stop=False)
            pe.matmul(mps[:, :], ones_n[:, :], fl[:, :, 4], start=False, stop=True).then_inc(mean_ready, 1)
            pe.wait_ge(steps, 7)
            pe.matmul(vps[:, :], ones_n[:, :], dev[:, 0, :], start=True, stop=True).then_inc(var_ready, 1)

        @block.scalar
        def _(act):
            act.wait_ge(steps, 8)
            act.activation(sd[:, :], m2[:, :], ACT.Sqrt).then_inc(sd_ready, 1)


def setup(nc, d, s, rows_dram):
    with ExitStack() as ctx:
        raw = ctx.enter_context(nc.sbuf_tensor("bias_raw", [1, 4, C], F32))
        rest = ctx.enter_context(nc.sbuf_tensor("bias_rest", [1, 4, C], F32))
        parts = ctx.enter_context(nc.sbuf_tensor("bias_parts", [1, 3, 4, C], BF16))
        kmraw = ctx.enter_context(nc.sbuf_tensor("km_raw", [2 * TAPS * TAPS, 4 * CH], F32))
        kmsign = ctx.enter_context(nc.sbuf_tensor("km_sign", [2 * TAPS * TAPS, 4 * CH], F32))
        taps = ctx.enter_context(nc.sbuf_tensor("taps", [C, 3, TAPS, TAPS], F32))
        rows = ctx.enter_context(nc.sbuf_tensor("rows", [C, 3, NQ + NWB - 1, RW], F32))
        loaded = ctx.enter_context(nc.semaphore("consts_in"))
        steps = ctx.enter_context(nc.semaphore("setup_steps"))
        placed = ctx.enter_context(nc.semaphore("parts_placed"))
        rows_out = ctx.enter_context(nc.semaphore("rows_out"))
        block = ctx.enter_context(nc.Block())

        @block.sync
        def _(sp):
            n = 0
            for dst, src in ((taps[:, :, :, :], d["taps"]), (raw[:, 0, :], d["bf"]), (raw[:, 1, :], d["bi"]),
                             (raw[:, 2, :], d["bd"]), (raw[:, 3, :], d["b_out"]),
                             (kmraw[:, :], d["km"]), (kmsign[:, :], d["km_sign"]),
                             (s["wfi"][:, 0:C], d["Wf"]), (s["wfi"][:, C:2 * C], d["Wi"]), (s["wd"][:, :], d["Wd"]),
                             (s["wout"][:, :], d["W_out"]), (s["ident"][:, :], d["ident"]),
                             (s["mask"][:, :], d["mask"]), (s["apad"][0:NWB * OH, :, :, :], d["apad"]), (s["count"][:, :, :], d["count"])):
                sp.dma_start(dst, src).then_inc(loaded, 16)
                n += 16
            assert n == 15 * 16
            sp.wait_ge(steps, 18)
            for k in range(3):
                for r in range(2):
                    sp.dma_start(s["b_fi"][k:k + 1, r, :], parts[:, k, 0:2, :].rearrange("p a c -> p (a c)")).then_inc(placed, 16)
                for r in range(4):
                    sp.dma_start(s["b_d"][k:k + 1, r, :], parts[:, k, 2, :]).then_inc(placed, 16)
                    sp.dma_start(s["b_o"][k:k + 1, r, :], parts[:, k, 3, :]).then_inc(placed, 16)
            sp.dma_start(rows_dram, rows[:, :, :, :].rearrange("c f q n -> c (f q n)")).then_inc(rows_out, 16)
            sp.wait_ge(placed, 3 * 10 * 16)
            sp.wait_ge(rows_out, 16)

        @block.vector
        def _(v):
            n = [0]

            def step(ins):
                ins.then_inc(steps, 1)
                n[0] += 1
                v.wait_ge(steps, n[0])

            step(v.memset(s["ones_n"][:, :], 1.0 / (2 * P)))
            step(v.memset(s["ones3"][:, :], 1.0))
            step(v.memset(s["tiny"][:, :], TINY))
            step(v.memset(rows[:, :, :, :], 0.0))
            v.wait_ge(loaded, 15 * 16)
            for f in range(3):
                step(v.tensor_copy(rows[:, f, NWB:NWB + TAPS, OH - 1:OH - 1 + TAPS], taps[:, f, :, :]))
            step(v.tensor_scalar(raw[:, 0, :], raw[:, 0, :], 2.0, None, ALU.add))
            step(v.tensor_copy(parts[:, 0, :, :], raw[:, :, :]))
            step(v.tensor_tensor(rest[:, :, :], raw[:, :, :], parts[:, 0, :, :], ALU.subtract))
            step(v.tensor_copy(parts[:, 1, :, :], rest[:, :, :]))
            step(v.tensor_tensor(raw[:, :, :], rest[:, :, :], parts[:, 1, :, :], ALU.subtract))
            step(v.tensor_copy(parts[:, 2, :, :], raw[:, :, :]))
            step(v.tensor_tensor(s["km"][:, :], kmraw[:, :], kmsign[:, :], ALU.mult))
            step(v.tensor_scalar(s["nident"][:, :], s["ident"][:, :], -1.0, None, ALU.mult))
            step(v.memset(s["half"][:, :], 0.5))
            step(v.memset(s["scale_o"][:, :], 1.0 - 2.0 ** -8))
            step(v.memset(s["bias_o"][:, :], 1e-6 * (1.0 - 2.0 ** -8)))


V_STEPS = ("m1 m2 fs p t d sp e g t2 b2 a1 v t4 s ep q er g1 y negx nry sy snx syt syd rx "
           "alpha av w n1 n2").split()
V = {n: i + 1 for i, n in enumerate(V_STEPS)}
KV = len(V_STEPS)
A_STEPS = "ev0 ev1 fi0 fi1 sd ln tt d2 t2t2 d4 sq4".split()
A = {n: i + 1 for i, n in enumerate(A_STEPS)}
KA = len(A_STEPS)
NSUB = 2 * SUBS


def layer0(nc, x, x1, basis, s):
    with ExitStack() as ctx:
        def sb(name, shape, dt=F32):
            return ctx.enter_context(nc.sbuf_tensor(name, shape, dt))

        def sem(name):
            return ctx.enter_context(nc.semaphore(name))

        xt = [sb(f"xt{i}", [P, WB, C]) for i in range(2)]
        ot = sb("ot", [P, C, WB])
        tab = {n: sb(f"tab_{n}", [P, WB * CH]) for n in ("Ar", "Ai", "A2", "Br", "Bi")}
        xnT = [sb(f"xnT{i}", [P, SW, P]) for i in range(2)]
        fi = [sb(f"fi{i}", [P, SW, 2 * C]) for i in range(2)]
        ld = [sb(f"ld{i}", [P, FULL]) for i in range(2)]
        NT = 21
        tmp = sb("tmp", [P, NT, HALF])
        ebuf = tmp[0:2 * TAPS * TAPS, 12:20, :].rearrange("p a n -> p (a n)").rearrange("p (w h) -> p w h", h=P)
        m1, m2, n1, n2, sp_, vv, av, fm = (sb(n, [P, FULL]) for n in ("m1", "m2", "n1", "n2", "spg", "vv", "av", "fm"))
        scale, shift = ([sb(f"{n}{i}", [C, 1]) for i in range(2)] for n in ("scale", "shift"))
        pT = ctx.enter_context(nc.psum_tensor("pT", [P, 2, 512], F32))
        pZ = ctx.enter_context(nc.psum_tensor("pZ", [P, 4, 512], F32))
        pD = ctx.enter_context(nc.psum_tensor("pD", [P, 2, 512], F32))
        x_in, x1_out, e_in = [sem(f"x_in{i}") for i in range(2)], sem("x1_out"), sem("e_in")
        pe_xT, pe_z, pe_xn, pe_bx, pe_m, pe_fin, pe_beta = (
            sem(n) for n in ("pe_xT", "pe_z", "pe_xn", "pe_bx", "pe_m", "pe_fin", "pe_beta"))
        v_done, a_done, fm_done, out_done = sem("v_done"), sem("a_done"), sem("fm_done"), sem("out_done")
        scale_set = sem("scale_set")
        tab_pe, tab_v, tab_a = sem("tab_pe"), sem("tab_v"), sem("tab_a")
        block = ctx.enter_context(nc.Block())

        (t, d, tt, d2, e, t2, t2t2, t4, d4, sq4, b2, a1, ss, q, er, ep, g1, y, negx, nry, rx) = (
            tmp[:, i, :] for i in range(NT))

        def vn(sblk, name, back=0):
            return sblk * KV + ((2 - back) * KV + V[name])

        def an(sblk, name, back=0):
            return sblk * KA + ((2 - back) * KA + A[name])

        def xnn(sblk, j, back=0):
            return sblk * 2 + (4 - 2 * back + j + 1)

        def tail_n(sblk, back=0):
            return sblk + (3 - back)

        TV = 27
        TA = 2
        NIT = B * SUBS // NSUB

        def walk(eng, tables, front, middle, tail):
            with eng.Fori(0, NWB) as wb:
                def number(ip, k):
                    return wb * (B * SUBS) + (ip * NSUB + k)

                def body(ip, last):
                    for k in range(NSUB):
                        first = isinstance(ip, int) and ip == 0 and k == 0
                        middle(wb, number(ip, k), k, None if first else number(ip, k - 1), (k - 1) % NSUB)
                        if k < NSUB - 1:
                            front(wb, ip * 2 + (k + 1) // SUBS, wb * (B // 2) + ip, number(ip, k + 1), k + 1, number(ip, k))
                        elif not last:
                            front(wb, ip * 2 + 2, wb * (B // 2) + ip + 1, number(ip, k + 1), 0, number(ip, k))

                tables(wb)
                front(wb, 0, wb * (B // 2), number(0, 0), 0, None)
                body(0, False)
                with eng.Fori(1, NIT - 1) as ip:
                    body(ip, False)
                body(NIT - 1, True)
                tail(number(NIT - 1, NSUB - 1), NSUB - 1)

        @block.sync
        def _(sp):
            sp.sem_inc(x1_out, 48)
            with sp.Fori(0, NWB) as wb:
                def load(b, u):
                    sp.dma_start(xt[u][:, :, :],
                                 x.rearrange("b h (k r) c -> b r h k c", r=NWB)[bass.ds(b, 1), bass.ds(wb, 1)]
                                 .rearrange("a e h k c -> (a e h) k c")
                                 ).then_inc(x_in[u], 16)

                def store(b):
                    sp.wait_ge(out_done, tail_n((wb * B + b) * SUBS + SUBS - 1))
                    for row, h0, h1 in ((EDGE, 0, H), (0, H - EDGE, H), (H + EDGE, 0, HPAD - H - EDGE)):
                        dst = x1[:, row:row + h1 - h0, bass.ds(b, 1), bass.ds(wb, 1), :, :].rearrange("g h a e c w -> h g (a e c w)")
                        sp.dma_start(dst, ot[h0:h1, :, :].rearrange("p (g c) w -> p g (c w)", g=G)).then_inc(x1_out, 16)

                sp.wait_ge(tab_pe, wb * 4 + 1)
                sp.dma_start(ebuf, basis[:, bass.ds(wb * WB, WB), :]).then_inc(e_in, 16)
                for u in range(2):
                    load(u, u)
                with sp.Fori(0, B // 2 - 1) as ip:
                    for u in range(2):
                        store(ip * 2 + u)
                        load(ip * 2 + (2 + u), u)
                for u in range(2):
                    store(B - 2 + u)
            sp.wait_ge(x1_out, 48 * (TILES + 1))

        @block.tensor
        def _(pe):
            pe.sem_inc(pe_xn, 4)
            pe.sem_inc(pe_fin, 2)
            pe.sem_inc(pe_m, 2)
            pe.sem_inc(tab_pe, 1)

            def tables(wb):
                pe.wait_ge(e_in, (wb + 1) * 16)
                pe.wait_ge(out_done, tail_n(wb * (B * SUBS), back=1))
                for j in range(4):
                    pe.wait_ge(tab_v, wb * TV + (4 * j + 1))
                    for w in range(SW):
                        last = pe.matmul(pZ[:, w // 2, (w % 2) * 256:(w % 2) * 256 + 256],
                                         ebuf[:, j * SW + w, :], s["km"][:, :], start=True, stop=True)
                    last.then_inc(tab_pe, 1)
                pe.wait_ge(tab_v, wb * TV + (16 + 1))

            def front(wb, b, pair, sblk, k, before):
                par, u, kt = k % 2, k // SUBS, k % SUBS
                if kt == 0:
                    pe.wait_ge(x_in[u], (pair + 1) * 16)
                pe.wait_ge(v_done, vn(sblk, "v", back=1))
                for j in range(2):
                    for w in range(4):
                        last = pe.transpose(pT[:, j, w * P:(w + 1) * P], xt[u][:, kt * SW + 4 * j + w, :], s["ident"][:, :])
                    last.then_inc(pe_xT, 1)
                pe.wait_ge(fm_done, tail_n(sblk, back=2))
                pe.wait_ge(out_done, tail_n(sblk, back=2))
                for j in range(2):
                    pe.wait_ge(a_done, an(sblk, f"ev{j}"))
                    for bank in (2 * j, 2 * j + 1):
                        pe.matmul(pZ[:, bank, :], s["ones3"][0:3, :], s["b_fi"][0:3, :, :], start=True, stop=False)
                        for w in (2 * bank, 2 * bank + 1):
                            last = pe.matmul(pZ[:, bank, (w % 2) * 256:(w % 2) * 256 + 256], xnT[par][:, w, :],
                                             s["wfi"][:, :], start=False, stop=w % 2 == 1)
                    last.then_inc(pe_z, 1)
                if before is not None:
                    beta_sum(before)
                pe.wait_ge(v_done, vn(sblk, "sp", back=1))
                for bank in range(2):
                    pe.matmul(pD[:, bank, :], s["ones3"][0:3, :], s["b_d"][0:3, :, :], start=True, stop=False)
                    for w in range(4):
                        last = pe.matmul(pD[:, bank, w * C:(w + 1) * C], xnT[par][:, 4 * bank + w, :],
                                         s["wd"][:, :], start=False, stop=w == 3)
                last.then_inc(pe_z, 1)
                pe.wait_ge(v_done, vn(sblk, "w", back=1))
                for j in range(2):
                    for w in range(4):
                        last = pe.transpose(pT[:, j, w * P:(w + 1) * P], xnT[par][:, 4 * j + w, :], s["ident"][:, :])
                    last.then_inc(pe_xn, 1)

            def part(ap, i):
                return view(ap[:, i * CH:i * CH + 1], [C, SW], [1, CH])

            def complex_sum(ps, a, b):
                pe.matmul(ps[:, 0, :], s["ident"][:, :], part(a, 0), start=True, stop=False)
                pe.matmul(ps[:, 0, :], s["nident"][:, :], part(b, 1), start=False, stop=True)
                pe.matmul(ps[:, 1, :], s["ident"][:, :], part(a, 1), start=True, stop=False)
                return pe.matmul(ps[:, 1, :], s["ident"][:, :], part(b, 0), start=False, stop=True)

            def beta_sum(sblk):
                pe.wait_ge(v_done, vn(sblk, "syt"))
                pe.matmul(pT[:, 0, :], s["ident"][:, :], t2t2, start=True, stop=False)
                pe.matmul(pT[:, 0, :], s["nident"][:, :], nry, start=False, stop=False)
                pe.matmul(pT[:, 0, :], s["nident"][:, :], g1, start=False, stop=True).then_inc(pe_beta, 1)

            def m_sum(sblk):
                pe.wait_ge(v_done, vn(sblk, "n2"))
                complex_sum(pZ, n1, n2).then_inc(pe_m, 1)

            def add_up(k, srcs, start, stop):
                u, kt = k // SUBS, k % SUBS
                for j in range(2):
                    for src in srcs:
                        rhs = (xt[u][:, kt * SW + 4 * j:kt * SW + 4 * j + 4, :].rearrange("p w c -> p (w c)") if src is xt
                               else src[:, j * 512:(j + 1) * 512])
                        last = pe.matmul(pZ[:, 2 + j, :], s["ident"][:, :], rhs, start=start and src is srcs[0],
                                         stop=stop and src is srcs[-1])
                return last

            def middle(wb, sblk, k, before, kb):
                pe.wait_ge(a_done, an(sblk, "fi1"))
                if before is not None:
                    m_sum(before)
                pe.wait_ge(v_done, vn(sblk, "m2"))
                complex_sum(pT, m1, m2).then_inc(pe_bx, 1)
                if before is not None:
                    add_up(kb, (av, xt), True, False)
                    pe.wait_ge(fm_done, tail_n(before))
                    add_up(kb, (fm,), False, True).then_inc(pe_fin, 1)

            def tail(sblk, k):
                beta_sum(sblk)
                m_sum(sblk)
                pe.wait_ge(out_done, tail_n(sblk, back=1))
                add_up(k, (av, xt), True, False)
                pe.wait_ge(fm_done, tail_n(sblk))
                add_up(k, (fm,), False, True).then_inc(pe_fin, 1)

            walk(pe, tables, front, middle, tail)

        @block.scalar
        def _(act):
            act.sem_inc(a_done, 2 * KA)
            act.sem_inc(out_done, 2)

            def tables(wb):
                act.wait_ge(tab_v, wb * TV + (1 + 19))
                mag = tmp[:, 0:4, :].rearrange("p a n -> p (a n)")
                sg = tmp[:, 4:8, :].rearrange("p a n -> p (a n)")
                act.activation(mag, tab["A2"][:, :], ACT.Sqrt).then_inc(tab_a, 1)
                act.wait_ge(tab_a, wb * TA + 1)
                act.activation(sg, mag, ACT.Sigmoid).then_inc(tab_a, 1)

            def front(wb, b, pair, sblk, k, before):
                par, u, kt = k % 2, k // SUBS, k % SUBS
                if kt == 0:
                    for src, dst in ((s["rstd"], scale), (s["nmr"], shift)):
                        act.activation(dst[u][:, :], src[:, bass.ds(b, 1)], ACT.Copy).then_inc(scale_set, 1)
                    act.wait_ge(scale_set, (pair * 2 + u) * 2 + 2)
                for j in range(2):
                    act.wait_ge(pe_xT, sblk * 2 + (j + 1))
                    act.wait_ge(pe_xn, xnn(sblk, 1, back=2))
                    act.activation(xnT[par][:, 4 * j:4 * j + 4, :].rearrange("p a n -> p (a n)"), pT[:, j, :], ACT.Identity,
                                   bias=shift[u][:, :], scale=scale[u][:, :]).then_inc(a_done, 1)
                act.wait_ge(fm_done, tail_n(sblk, back=2))
                for j in range(2):
                    act.wait_ge(pe_z, sblk * 3 + (j + 1))
                    act.activation(fi[par][:, 4 * j:4 * j + 4, :].rearrange("p a n -> p (a n)"),
                                   pZ[:, 2 * j:2 * j + 2, :].rearrange("p a n -> p (a n)"), ACT.Sigmoid).then_inc(a_done, 1)
                act.wait_ge(pe_z, sblk * 3 + 3)
                act.activation(ld[par][:, :], pD[:, :, :].rearrange("p a n -> p (a n)"), ACT.Sigmoid, scale=-1.0).then_inc(a_done, 1)
                act.wait_ge(a_done, an(sblk, "sd"))
                act.activation(ld[par][:, :], ld[par][:, :], ACT.Ln, bias=s["tiny"][:, :]).then_inc(a_done, 1)

            def take(sblk, k):
                kt = k % SUBS
                act.wait_ge(pe_fin, tail_n(sblk))
                if kt == 0:
                    act.wait_ge(x1_out, sblk * (48 // SUBS) + 48)
                act.activation(view(ot[:, 0, kt * SW:kt * SW + 1], [1, SW], [WB, C]),
                               pZ[:, 2:4, :].rearrange("p a (w c) -> p (a w) c", c=C), ACT.Copy).then_inc(out_done, 1)

            def middle(wb, sblk, k, before, kb):
                for name, src, dst in (("t", t, tt), ("d", d, d2), ("t2", t2, t2t2), (None, d2, d4)):
                    if name:
                        act.wait_ge(v_done, vn(sblk, name))
                    else:
                        act.wait_ge(a_done, an(sblk, "d2"))
                    act.activation(dst, src, ACT.Square).then_inc(a_done, 1)
                act.wait_ge(v_done, vn(sblk, "t4"))
                act.activation(sq4, t4, ACT.Square, bias=s["half"][:, :]).then_inc(a_done, 1)
                if before is not None:
                    take(before, kb)

            walk(act, tables, front, middle, take)

        @block.vector
        def _(v):
            v.sem_inc(v_done, 2 * KV)
            v.sem_inc(fm_done, 2)
            v.sem_inc(tab_v, 1)
            tts, tsc = v.tensor_tensor, v.scalar_tensor_tensor

            def tables(wb):
                count = [0]

                def step(ins, wait=True):
                    ins.then_inc(tab_v, 1)
                    count[0] += 1
                    if wait:
                        v.wait_ge(tab_v, wb * TV + (1 + count[0]))

                mag, sg, rc = (tmp[:, 4 * i:4 * i + 4, :].rearrange("p a n -> p (a n)") for i in range(3))
                Ar, Ai, A2 = tab["Ar"][:, :], tab["Ai"][:, :], tab["A2"][:, :]
                v.wait_ge(v_done, vn(wb * (B * SUBS), "n2", back=1))
                for j in range(4):
                    v.wait_ge(tab_pe, wb * 4 + (2 + j))
                    for i, name in enumerate(("Ar", "Ai", "Br", "Bi")):
                        step(v.tensor_scalar(tab[name][:, j * HALF:(j + 1) * HALF].rearrange("p (w c) -> p w c", c=CH),
                                             view(pZ[:, 0, i * CH:i * CH + 1], [256, SW], [1, CH]),
                                             1.0 if i < 2 else 0.1, None, ALU.mult), wait=i == 3)
                step(tts(rc, Ai, Ai, ALU.mult), wait=False)
                step(tts(A2, Ar, Ar, ALU.mult))
                step(tsc(A2, A2, 1e-8, rc, ALU.add, ALU.add))
                v.wait_ge(tab_a, wb * TA + 2)
                step(v.tensor_scalar(mag, mag, 1e-8, None, ALU.add))
                step(v.reciprocal(rc, mag))
                step(tsc(rc, sg, 0.95, rc, ALU.mult, ALU.mult))
                step(tts(Ar, Ar, rc, ALU.mult), wait=False)
                step(tts(Ai, Ai, rc, ALU.mult))
                step(tts(rc, Ai, Ai, ALU.mult), wait=False)
                step(tts(A2, Ar, Ar, ALU.mult))
                step(tts(A2, A2, rc, ALU.add), wait=False)
                assert count[0] == TV

            def pair(ap):
                return view(ap, [CH, SW], [0, 2], [1, CH])

            def w2c(ap):
                return view(ap, [C, SW], [CH, 2], [1, CH])

            def banks(ps):
                return view(ps[:, 0, 0:1], [CH, SW], [512, 2], [1, CH])

            def wc(ap):
                return ap.rearrange("p (w c) -> p w c", c=C)

            def apply_f(sblk, k):
                v.wait_ge(pe_m, tail_n(sblk))
                v.wait_ge(pe_fin, tail_n(sblk, back=1))
                tts(w2c(fm[:, :]), view(fi[k % 2][:, 0, 0:1], [2 * C, SW], [CH, 2], [1, CH]), banks(pZ), ALU.mult).then_inc(fm_done, 1)

            def front(*_):
                pass

            def middle(wb, sblk, k, before, kb):
                par, u, kt = k % 2, k // SUBS, k % SUBS
                last = [0]

                def step(name, ins_fn, follows=False):
                    assert V_STEPS[last[0]] == name, name
                    v.wait_ge(v_done, sblk * KV + (2 * KV + last[0] - (0 if follows else 1)))
                    ins_fn().then_inc(v_done, 1)
                    last[0] += 1

                cols = slice(kt * HALF, (kt + 1) * HALF)
                Ar, Ai, A2, Br, Bi = (tab[n][:, cols] for n in ("Ar", "Ai", "A2", "Br", "Bi"))
                i_full = fi[par][:, :, C:2 * C]
                fr, fim = fi[par][:, :, 0:CH], fi[par][:, :, CH:C]
                xn = pT[:, :, :].rearrange("p a n -> p (a n)")
                M1, M2, N1, N2, SP, VV, AV = (z[:, :] for z in (m1, m2, n1, n2, sp_, vv, av))
                if before is None:
                    v.wait_ge(tab_v, wb * TV + (TV + 1))
                v.wait_ge(pe_xn, xnn(sblk, 1))
                step("m1", lambda: tts(w2c(M1), w2c(xn), pair(Br), ALU.mult), True)
                step("m2", lambda: tts(w2c(M2), w2c(xn), pair(Bi), ALU.mult))
                v.wait_ge(a_done, an(sblk, "fi1"))
                step("fs", lambda: tts(b2.rearrange("p (w c) -> p w c", c=CH), fr, fim, ALU.add))
                step("p", lambda: tts(a1.rearrange("p (w c) -> p w c", c=CH), fr, fim, ALU.mult))
                step("t", lambda: tts(t, b2, Ar, ALU.mult))
                step("d", lambda: tts(d, a1, A2, ALU.mult))
                v.wait_ge(a_done, an(sblk, "ln"))
                step("sp", lambda: tsc(SP, ld[par][:, :], -1.0, pD[:, :, :].rearrange("p a n -> p (a n)"), ALU.mult, ALU.max))
                if before is not None:
                    apply_f(before, kb)
                v.wait_ge(a_done, an(sblk, "tt"))
                step("e", lambda: tts(e, tt, d, ALU.subtract))
                step("g", lambda: tts(wc(SP), wc(SP), i_full, ALU.mult))
                step("t2", lambda: tts(t2, e, d, ALU.subtract))
                step("b2", lambda: tts(b2, e, d, ALU.mult))
                step("a1", lambda: tts(a1, t2, t, ALU.mult))
                v.wait_ge(pe_bx, sblk + 1)
                step("v", lambda: tts(w2c(VV), w2c(SP), banks(pT), ALU.mult))
                v.wait_ge(a_done, an(sblk, "t2t2"))
                step("t4", lambda: tsc(t4, d2, -2.0, t2t2, ALU.mult, ALU.add))
                step("s", lambda: tsc(ss, t, 1.0, e, ALU.add, ALU.add))
                v.wait_ge(a_done, an(sblk, "d4"))
                step("ep", lambda: tsc(ep, t4, 1.0, d4, ALU.add, ALU.mult))
                v.wait_ge(a_done, an(sblk, "sq4"))
                step("q", lambda: tsc(q, sq4, 0.75, d4, ALU.add, ALU.subtract))
                step("er", lambda: tsc(er, t, 1.0, d, ALU.add, ALU.mult))
                step("g1", lambda: tts(g1, q, b2, ALU.mult))
                step("y", lambda: tts(y, q, a1, ALU.mult))
                step("negx", lambda: tsc(negx, ep, -1.0, g1, ALU.add, ALU.add))
                step("nry", lambda: tsc(nry, er, -1.0, y, ALU.add, ALU.mult))
                step("sy", lambda: tts(ep, ss, y, ALU.mult))
                step("snx", lambda: tts(g1, ss, negx, ALU.mult))
                step("syt", lambda: tts(t2t2, ep, t, ALU.mult))
                step("syd", lambda: tts(t2, ep, d, ALU.mult))
                step("rx", lambda: tsc(rx, er, -1.0, negx, ALU.add, ALU.mult))
                step("alpha", lambda: tts(rx, rx, t2, ALU.subtract), True)
                v.wait_ge(pe_fin, tail_n(sblk, back=1))
                step("av", lambda: tts(w2c(AV), pair(rx), w2c(VV), ALU.mult), True)
                v.wait_ge(pe_beta, sblk + 1)
                step("w", lambda: tts(w2c(SP), pair(pT[:, 0, :]), w2c(VV), ALU.mult))
                step("n1", lambda: tts(w2c(N1), w2c(SP), pair(Ar), ALU.mult), True)
                step("n2", lambda: tts(w2c(N2), w2c(SP), pair(Ai), ALU.mult))
                assert last[0] == KV

            walk(v, tables, front, middle, apply_f)


def channel_steps(last):
    dve, act = [], []
    for cc in range(CG):
        prep = not (last and cc == CG - 1)

        def of(names, yes=True):
            return [f"{n}{cc}" for n in names.split()] if yes else []

        bn = [[] if last else [f"bn{p}_{b}" for b in part for p in range(2)] for part in BN_PARTS[cc]]
        stats = not last and cc == 2
        dve += (["rs"] if not last and cc == 3 else []) + of("xs xm hl hr", prep) + of("bt0_ bt1_") + bn[0] + of("at")
        dve += ["mean", "de", "do", "m2", "dq", "ds", "vs0", "vs1"] if stats else []
        dve += of("tl", prep) + (["ve"] if stats else []) + of("xl", prep) + of("bt2_ bt3_ c2_ c4_ f0_ f1_ f2_") + bn[1] + of("bt4_")
        act += of("z0_ z1_ ga") + of("ta th xh", prep) + of("z2_ z3_ s1_ c1_") + (["sq"] if stats else []) + of("z4_ sb ln")
    return dve, act


BN_PARTS = (((0, 1, 2), (3, 4, 5, 6)), ((7, 8, 9), (10, 11, 12, 13)), ((14, 15), ()), ((), ()))
NO = NWB * OH


def layer1_conv(nc, x1, hs, rows_dram, s):
    XW = WB + 2
    RWIN = (NQ - 1) * RW + OH
    with ExitStack() as ctx:
        def sb(name, shape, dt=F32):
            return ctx.enter_context(nc.sbuf_tensor(name, shape, dt))

        def sem(name):
            return ctx.enter_context(nc.semaphore(name))

        xg = [sb(f"xg{i}", [P, B, HB, CG, WB]) for i in range(2)]
        traw = [sb(f"traw{i}", [P, 3, RWIN]) for i in range(2)]
        thi = [sb(f"thi{i}", [P, 2, NQ * OH], F32R) for i in range(2)]
        tlo = [sb(f"tlo{i}", [P, 2, NQ * OH], F32R) for i in range(2)]
        ta = sb("ta", [P, NQ * OH])
        xn = sb("xn", [P, HB, B, XW])
        xhi = [sb(f"xhi{i}", [P, HB, B, XW], F32R) for i in range(2)]
        xlo = [sb(f"xlo{i}", [P, HB, B, XW], F32R) for i in range(2)]
        gate = sb("gate", [P, HB, B, WB])
        bt = sb("bt", [P, HB, B, WB])
        oc = [sb(f"oc{i}", [P, HB, B, WB]) for i in range(2)]
        st = sb("st1", [P, 2, B, 6])
        mean = sb("mean1", [P, B])
        rstd = sb("rstd1", [P, B])
        dev = sb("dev1", [P, 2, 2, B])
        vs = sb("vs1", [P, 2, B])
        ve = sb("ve1", [P, B])
        sq = sb("sq1", [P, B])
        at, ff, c1, c2, c4, fx = (sb(n, [P, 2, B, 2]) for n in ("at", "ff", "c1", "c2", "c4", "fx"))
        pG = ctx.enter_context(nc.psum_tensor("pG", [P, 3, 512], F32))
        pB = ctx.enter_context(nc.psum_tensor("pB", [P, 3, 512], F32))
        pA = ctx.enter_context(nc.psum_tensor("pA", [P, 512], F32))
        pS = ctx.enter_context(nc.psum_tensor("pS", [P, 512], F32))
        pe_zg, pe_zb, pe_ga, pe_mean, pe_var = (sem(n) for n in ("pe_zg", "pe_zb", "pe_ga", "pe_mean", "pe_var"))
        v_done, a_done, v_tail, a_tail = sem("cv_done"), sem("ca_done"), sem("cv_tail"), sem("ca_tail")
        xg_in, t_in, hs_out = ([sem(f"{n}{i}") for i in range(2)] for n in ("xg_in", "t_in", "hs_out"))
        first_v, first_a, first_p = sem("first_v"), sem("first_a"), sem("first_p")
        block = ctx.enter_context(nc.Block())

        names = {last: channel_steps(last) for last in (False, True)}
        place = {last: [{n: i + 1 for i, n in enumerate(x)} for x in names[last]] for last in (False, True)}
        KV1, KA1 = (len(x) for x in names[False])
        XG, TI, HO = NWB * 16, NWB * 16, HB * 16

        def vc(g, name, last=False, back=0):
            return g * KV1 + ((1 - back) * KV1 + place[last][0][name])

        def ac(g, name, last=False, back=0):
            return g * KA1 + ((1 - back) * KA1 + place[last][1][name])

        def units(g, cc):
            return (g * CG + (cc + 1)) * HB

        def chan(g, cc, n):
            return g * CG + (cc + n)

        def groups(eng, do, peeled=1):
            do(0, 0, 0, True, False)
            with eng.Fori(0, (G - 1 - peeled) // 2) as i:
                for gp in (1, 2):
                    do(i * 2 + gp, gp % 2, i + 1, False, False)
            for g in range(G - peeled, G):
                do(g, g % 2, (g + 1) // 2, False, g == G - 1)

        @block.sync
        def _(sp):
            for i in range(2):
                sp.sem_inc(hs_out[i], HO)

            def load_group(g, par):
                for r in range(NWB):
                    src = x1[bass.ds(g, 1), 0:IH, :, r, :, :]
                    src = bass.AP(src.tensor, src.offset,
                                  [[B * NWB * CG * WB, IH], [NWB * CG * WB, B], [OH * B * NWB * CG * WB, HB], [1, CG * WB]])
                    p0 = (NWB - 1 - r) * IH
                    sp.dma_start(xg[par][p0:p0 + IH, :, :, :, :].rearrange("p b e c w -> p b e (c w)"), src).then_inc(xg_in[par], 16)

            def load_taps(c, par):
                for r in range(NWB):
                    base = rows_dram[bass.ds(c, 1), :]
                    src = bass.AP(base.tensor, base.offset + r * RW, [[1, IH], [(NQ + NWB - 1) * RW, 3], [1, RWIN]])
                    sp.dma_start(traw[par][r * IH:(r + 1) * IH, :, :], src).then_inc(t_in[par], 16)

            def store(c, par):
                for hb in range(HB):
                    base = hs[bass.ds(c, 1), (HB - 1 - hb) * OH:(HB - hb) * OH, :, :]
                    dst = bass.AP(base.tensor, base.offset, [[B * WB, NWB], [NWB * B * WB, OH], [1, B * WB]])
                    sp.dma_start(dst, oc[par][0:NO, hb, :, :].rearrange("p b w -> p (b w)")).then_inc(hs_out[par], 16)

            load_group(0, 0)
            for i in range(2):
                load_taps(i, i)
            load_group(1, 1)

            def do(g, gpar, half, first, last):
                more = not isinstance(g, int) or g < G - 2
                for cc in range(CG):
                    if not (last and cc >= 2):
                        sp.wait_ge(pe_ga, chan(g, cc, 2))
                        load_taps(chan(g, cc, 2), cc % 2)
                    if cc == 2 and more:
                        sp.wait_ge(v_done, vc(g, "xs2"))
                        load_group(g + 2, gpar)
                    if not (first and cc == 0):
                        sp.wait_ge(a_tail, chan(g, cc, 1) * 3)
                        store(chan(g, cc, -1), (cc + 1) % 2)

            groups(sp, do, 3)
            sp.wait_ge(a_tail, (C + 1) * 3)
            store(C - 1, 1)
            for i in range(2):
                sp.wait_ge(hs_out[i], HO * (C // 2 + 1))

        @block.tensor
        def _(pe):
            pe.sem_inc(pe_zg, HB)
            pe.sem_inc(pe_zb, HB)
            pe.sem_inc(pe_ga, 1)
            pe.sem_inc(pe_mean, 1)
            pe.sem_inc(pe_var, 1)

            def mean_mm():
                for part in range(2):
                    for f in (1, 4):
                        last = pe.matmul(pS[:, 0:B], s["count"][:, part, :], st[:, part, :, f],
                                         start=part == 0 and f == 1, stop=part == 1 and f == 4)
                return last

            def var_mm():
                pe.matmul(pS[:, 0:B], s["count"][:, 0, :], vs[:, 0, :], start=True, stop=False)
                return pe.matmul(pS[:, 0:B], s["count"][:, 1, :], vs[:, 1, :], start=False, stop=True)

            pe.wait_ge(first_v, 2 * B)
            mean_mm().then_inc(first_p, 1)
            pe.wait_ge(first_v, 2 * B + 8)
            var_mm().then_inc(first_p, 1)

            def conv(ps, f, par, hb):
                for dist in range(3):
                    for t, xs in ((thi, xhi), (thi, xlo), (tlo, xhi)):
                        last = pe.matmul(ps[0:NO, hb % 3, :], t[par][:, f, dist * NO:(dist + 1) * NO],
                                         xs[par][:, hb, :, 2 - dist:2 - dist + WB],
                                         start=dist == 0 and t is thi and xs is xhi, stop=dist == 2 and t is tlo)
                return last

            def do(g, gpar, half, first, last):
                for cc in range(CG):
                    par = cc % 2
                    pe.wait_ge(v_done, vc(g, "xl3", back=1) if cc == 0 else vc(g, f"xl{cc - 1}", last))
                    pe.wait_ge(a_done, ac(g, "ga3", back=1) if cc == 0 else ac(g, f"ga{cc - 1}", last))
                    for dist in range(3):
                        m = pe.matmul(pA[0:NO, 0:4 * B], ta[:, dist * NO:(dist + 1) * NO],
                                      view(xn[:, 0, 0, 2 - dist:3 - dist], [(HB - 1) * B * XW, 2], [XW, B], [WB - 1, 2]),
                                      start=dist == 0, stop=dist == 2)
                    m.then_inc(pe_ga, 1)
                    for hb in range(HB):
                        if hb >= 3:
                            pe.wait_ge(v_done, vc(g, f"bt{hb - 3}_{cc}", last))
                        else:
                            before = (3, 4, 2)[hb]
                            pe.wait_ge(v_done, vc(g, f"bt{before}_3", back=1) if cc == 0 else vc(g, f"bt{before}_{cc - 1}", last))
                        conv(pG, 0, par, hb).then_inc(pe_zg, 1)
                        if cc == 2 and not last and hb == 3:
                            pe.wait_ge(v_done, vc(g, f"bn1_{B - 1}"))
                            mean_mm().then_inc(pe_mean, 1)
                        if cc == 2 and not last and hb == 4:
                            pe.wait_ge(v_done, vc(g, "vs1"))
                            var_mm().then_inc(pe_var, 1)
                        conv(pB, 1, par, hb).then_inc(pe_zb, 1)

            groups(pe, do)

        @block.scalar
        def _(act):
            def split_x(par):
                return act.activation(xhi[par][:, :, :, :].rearrange("p e b w -> p (e b w)"),
                                      xn[:, :, :, :].rearrange("p e b w -> p (e b w)"), ACT.Copy)

            def split_t(par):
                return act.activation(thi[par][:, :, :].rearrange("p f (q m) -> p f q m", m=OH),
                                      view(traw[par][:, 0, 0:1], [RWIN, 2], [RW, NQ], [1, OH]), ACT.Copy)

            def pack_a(par):
                return act.activation(ta[:, :].rearrange("p (q m) -> p q m", m=OH),
                                      view(traw[par][:, 2, 0:1], [RW, NQ], [1, OH]), ACT.Copy)

            act.wait_ge(first_v, 2 * B + 9)
            act.activation(sq[:, :], ve[:, :], ACT.Sqrt).then_inc(first_a, 1)
            act.wait_ge(first_v, 2 * B + 14)
            split_x(0).then_inc(first_a, 1)
            act.wait_ge(t_in[0], TI)
            pack_a(0).then_inc(first_a, 1)
            split_t(0).then_inc(first_a, 1)
            act.sem_inc(a_done, KA1)
            act.sem_inc(a_tail, 3)

            def tail(n, par):
                act.wait_ge(v_tail, n * 3 + 3)
                act.activation(oc[par][0:NO, :, :, :].rearrange("p e b w -> p (e b w)"),
                               oc[par][0:NO, :, :, :].rearrange("p e b w -> p (e b w)"), ACT.Identity,
                               bias=s["bias_o"][0:NO, :], scale=s["scale_o"][0:NO, :]).then_inc(a_tail, 1)
                act.wait_ge(a_tail, n * 3 + 4)
                for i in range(2):
                    act.activation(view(oc[par][0:NO, i * (HB - 1), 0, 0:1], [WB, B], [WB - 1, 2]), fx[0:NO, i, :, :],
                                   ACT.Copy).then_inc(a_tail, 1)

            def do(g, gpar, half, first, last):
                done = [0]
                order = names[last][1]

                def step(name, ins):
                    assert order[done[0]] == name, (order[done[0]], name)
                    ins.then_inc(a_done, 1)
                    done[0] += 1

                for cc in range(CG):
                    par, nxt = cc % 2, (cc + 1) % 2
                    prep = not (last and cc == CG - 1)

                    def z(k):
                        act.wait_ge(pe_zg, units(g, cc) + (k + 1))
                        act.wait_ge(v_done, vc(g, f"bt{k}_3", back=1) if cc == 0 else vc(g, f"bt{k}_{cc - 1}", last))
                        step(f"z{k}_{cc}", act.activation(gate[0:NO, k, :, :].rearrange("p b w -> p (b w)"),
                                                          pG[0:NO, k % 3, :], ACT.Sigmoid))

                    z(0)
                    z(1)
                    act.wait_ge(pe_ga, chan(g, cc, 2))
                    step(f"ga{cc}", act.activation(at[0:NO, :, :, :].rearrange("p e b w -> p (e b w)"), pA[0:NO, 0:4 * B], ACT.Sigmoid))
                    if prep:
                        act.wait_ge(v_done, vc(g, f"hr{cc}", last))
                        act.wait_ge(pe_zb, units(g, cc))
                        act.wait_ge(t_in[nxt], (g * 2 + (1 + (cc + 1) // 2)) * TI)
                        step(f"ta{cc}", pack_a(nxt))
                        step(f"th{cc}", split_t(nxt))
                        step(f"xh{cc}", split_x(nxt))
                    z(2)
                    if not (first and cc == 0):
                        tail(chan(g, cc, -1), nxt)
                    z(3)
                    act.wait_ge(v_done, vc(g, f"at{cc}", last))
                    for name, dst, sign in (("s1_", ff, 1.0), ("c1_", c1, -1.0)):
                        step(f"{name}{cc}", act.activation(dst[0:NO, :, :, :].rearrange("p e b w -> p (e b w)"),
                                                           at[0:NO, :, :, :].rearrange("p e b w -> p (e b w)"), ACT.Sigmoid, scale=sign))
                    if cc == 2 and not last:
                        act.wait_ge(v_done, vc(g, "ve"))
                        step("sq", act.activation(sq[:, :], ve[:, :], ACT.Sqrt))
                    z(4)
                    act.wait_ge(v_done, vc(g, f"bt4_{cc}", last))
                    act.wait_ge(hs_out[par], (g * 2 + (1 + cc // 2)) * HO)
                    flat = oc[par][0:NO, :, :, :].rearrange("p e b w -> p (e b w)")
                    step(f"sb{cc}", act.activation(flat, bt[0:NO, :, :, :].rearrange("p e b w -> p (e b w)"), ACT.Sigmoid, scale=-1.0))
                    act.wait_ge(a_done, ac(g, f"sb{cc}", last))
                    step(f"ln{cc}", act.activation(flat, flat, ACT.Ln, bias=s["tiny"][0:NO, :]))
                assert done[0] == len(order)

            groups(act, do)
            tail(C - 1, 1)

        @block.vector
        def _(v):
            tts, tsc = v.tensor_tensor, v.scalar_tensor_tensor

            def bn(gpar, part, b):
                e = slice(0, HB - 1) if part == 0 else slice(HB - 1, HB)
                return v.bn_stats(st[:, part, b, :], xg[gpar][:, b, e, :, :].rearrange("p e c w -> p (e c w)"))

            def stats_mid():
                pmean = view(pS[:, 0:1], [0, 2], [1, B])
                yield "mean", lambda: v.tensor_copy(mean[:, :], pS[:, 0:B])
                yield "de", lambda: tts(dev[:, :, 0, :], st[:, :, :, 1], pmean, ALU.subtract)
                yield "do", lambda: tts(dev[:, :, 1, :], st[:, :, :, 4], pmean, ALU.subtract)
                yield "m2", lambda: tts(vs[:, :, :], st[:, :, :, 2], st[:, :, :, 5], ALU.add)
                yield "dq", lambda: tts(dev[:, :, :, :], dev[:, :, :, :], dev[:, :, :, :], ALU.mult)
                yield "ds", lambda: tts(dev[:, :, 0, :], dev[:, :, 0, :], dev[:, :, 1, :], ALU.add)
                for i, n in enumerate(((HB - 1) * CG * WB // 2, CG * WB // 2)):
                    yield f"vs{i}", lambda i=i, n=n: tsc(vs[:, i, :], vs[:, i, :], 1.0 / n, dev[:, i, 0, :], ALU.mult, ALU.add)

            def ve_():
                return v.tensor_scalar(ve[:, :], pS[:, 0:B], GN_EPS, None, ALU.add)

            def rs_():
                return v.reciprocal(rstd[:, :], sq[:, :])

            def norm(gpar, cc):
                mid = xn[:, :, :, 1:1 + WB]
                yield "xs", lambda: tts(mid, view(xg[gpar][:, 0, 0, cc, 0:1], [CG * WB, HB], [HB * CG * WB, B], [1, WB]),
                                        view(mean[:, 0:1], [0, HB], [1, B], [0, WB]), ALU.subtract)
                yield "xm", lambda: tts(mid, mid, view(rstd[:, 0:1], [0, HB], [1, B], [0, WB]), ALU.mult)
                yield "hl", lambda: v.tensor_copy(xn[:, :, :, 0:1], xn[:, :, :, WB:WB + 1])
                yield "hr", lambda: v.tensor_copy(xn[:, :, :, WB + 1:WB + 2], xn[:, :, :, 1:2])

            def low_x(par):
                return tts(xlo[par][:, :, :, :].rearrange("p e b w -> p (e b w)"), xn[:, :, :, :].rearrange("p e b w -> p (e b w)"),
                           xhi[par][:, :, :, :].rearrange("p e b w -> p (e b w)").bitcast(F32), ALU.subtract)

            def low_t(par):
                return tts(tlo[par][:, :, :].rearrange("p f (q m) -> p f q m", m=OH),
                           view(traw[par][:, 0, 0:1], [RWIN, 2], [RW, NQ], [1, OH]),
                           thi[par][:, :, :].rearrange("p f (q m) -> p f q m", m=OH).bitcast(F32), ALU.subtract)

            n = [0]

            def early(f):
                f().then_inc(first_v, 1)
                n[0] += 1
                v.wait_ge(first_v, n[0])

            v.wait_ge(xg_in[0], XG)
            for b in range(B):
                for part in range(2):
                    early(lambda: bn(0, part, b))
            v.wait_ge(first_p, 1)
            for name, f in stats_mid():
                early(f)
            v.wait_ge(first_p, 2)
            early(ve_)
            v.wait_ge(first_a, 1)
            early(rs_)
            for name, f in norm(0, 0):
                early(f)
            v.wait_ge(first_a, 4)
            early(lambda: low_x(0))
            early(lambda: low_t(0))
            assert n[0] == 2 * B + 16
            v.sem_inc(v_done, KV1)

            def tail(n, par, ln_count):
                v.wait_ge(a_done, ln_count)
                tsc(oc[par][0:NO, :, :, :].rearrange("p e b w -> p (e b w)"), oc[par][0:NO, :, :, :].rearrange("p e b w -> p (e b w)"),
                    -1.0, bt[0:NO, :, :, :].rearrange("p e b w -> p (e b w)"), ALU.mult, ALU.max).then_inc(v_tail, 1)
                v.wait_ge(v_tail, n * 3 + 1)
                v.wait_ge(a_tail, n * 3 + 3)
                for i in range(2):
                    tsc(fx[0:NO, i, :, :], view(oc[par][0:NO, i * (HB - 1), 0, 0:1], [WB, B], [WB - 1, 2]),
                        1e-6, ff[0:NO, i, :, :], ALU.add, ALU.mult).then_inc(v_tail, 1)

            def do(g, gpar, half, first, last):
                done = [0]
                order = names[last][0]

                def step(name, f, follows=True):
                    assert order[done[0]] == name, (order[done[0]], name)
                    v.wait_ge(v_done, g * KV1 + (KV1 + done[0] - (0 if follows else 1)))
                    f().then_inc(v_done, 1)
                    done[0] += 1

                for cc in range(CG):
                    par, nxt = cc % 2, (cc + 1) % 2
                    prep = not (last and cc == CG - 1)
                    stats = cc == 2 and not last
                    normal = norm((gpar + (cc == CG - 1)) % 2, (cc + 1) % CG)

                    def norm_steps(k):
                        for _ in range(k):
                            name, f = next(normal)
                            step(f"{name}{cc}", f)

                    def bt_(k):
                        v.wait_ge(pe_zb, units(g, cc) + (k + 1))
                        v.wait_ge(a_done, ac(g, f"z{k}_{cc}", last))
                        step(f"bt{k}_{cc}", lambda: tts(bt[0:NO, k, :, :].rearrange("p b w -> p (b w)"),
                                                        gate[0:NO, k, :, :].rearrange("p b w -> p (b w)"), pB[0:NO, k % 3, :], ALU.mult), False)

                    def bns(half):
                        if not last:
                            for b in BN_PARTS[cc][half]:
                                for part in range(2):
                                    step(f"bn{part}_{b}", lambda: bn((gpar + 1) % 2, part, b), False)

                    if cc == 3 and not last:
                        v.wait_ge(a_done, ac(g, "sq"))
                        step("rs", rs_)
                    if prep:
                        v.wait_ge(pe_ga, chan(g, cc, 2))
                        norm_steps(4)
                    if not (first and cc == 0):
                        tail(chan(g, cc, -1), nxt, ac(g, "ln3", back=1) if cc == 0 else ac(g, f"ln{cc - 1}", last))
                    bt_(0)
                    bt_(1)
                    if cc == 0 and not last:
                        v.wait_ge(xg_in[(gpar + 1) % 2], (half + 1) * XG)
                    bns(0)
                    v.wait_ge(a_done, ac(g, f"ga{cc}", last))
                    step(f"at{cc}", lambda: tts(at[0:NO, :, :, :], at[0:NO, :, :, :], apad_of(chan(g, cc, 0)), ALU.mult))
                    if stats:
                        v.wait_ge(pe_mean, g + 2)
                        for name, f in stats_mid():
                            step(name, f)
                    if prep:
                        v.wait_ge(a_done, ac(g, f"th{cc}", last))
                        step(f"tl{cc}", lambda: low_t(nxt))
                    if stats:
                        v.wait_ge(pe_var, g + 2)
                        step("ve", ve_)
                    if prep:
                        v.wait_ge(a_done, ac(g, f"xh{cc}", last))
                        step(f"xl{cc}", lambda: low_x(nxt))
                    bt_(2)
                    bt_(3)
                    fl = [q[0:NO, :, :, :].rearrange("p e b w -> p (e b w)") for q in (ff, c1, c2, c4)]
                    v.wait_ge(a_done, ac(g, f"c1_{cc}", last))
                    step(f"c2_{cc}", lambda: tts(fl[2], fl[1], fl[1], ALU.mult))
                    step(f"c4_{cc}", lambda: tts(fl[3], fl[2], fl[2], ALU.mult))
                    step(f"f0_{cc}", lambda: tsc(fl[0], fl[1], 1.0, fl[0], ALU.add, ALU.mult))
                    step(f"f1_{cc}", lambda: tsc(fl[0], fl[2], 1.0, fl[0], ALU.add, ALU.mult))
                    step(f"f2_{cc}", lambda: tsc(fl[0], fl[3], 1.0, fl[0], ALU.add, ALU.mult))
                    bns(1)
                    bt_(4)
                assert done[0] == len(order)

            def apad_of(c):
                a = s["apad"][0:NO, c, :, :] if isinstance(c, int) else s["apad"][0:NO, bass.ds(c, 1), :, :]
                return view(a, [2, 2], [0, B], [1, 2])

            groups(v, do)
            tail(C - 1, 1, ac(G - 1, "ln3", True))


def layer1_out(nc, x1, hs, y, s):
    NB = 4
    NQD = WB // 4
    NT = B // NB * NWB
    with ExitStack() as ctx:
        def sb(name, shape, dt=F32):
            return ctx.enter_context(nc.sbuf_tensor(name, shape, dt))

        def sem(name):
            return ctx.enter_context(nc.semaphore(name))

        ht = [sb(f"ht{i}", [P, C, NB * WB]) for i in range(2)]
        xt = [sb(f"x1t{i}", [P, C, WB]) for i in range(2)]
        yt = [sb(f"yt{i}", [P, WB, C]) for i in range(2)]
        hT = [sb(f"hT{i}", [P, 4, P]) for i in range(2)]
        pT = [ctx.enter_context(nc.psum_tensor(f"dT{i}", [P, 512], F32)) for i in range(2)]
        pO = [ctx.enter_context(nc.psum_tensor(f"dO{i}", [P, 512], F32)) for i in range(2)]
        h_in, x_in, y_out = ([sem(f"{n}{i}") for i in range(2)] for n in ("h_in", "x1_in", "y_out"))
        pe_T, pe_O, a_done, v_done = sem("pe_T"), sem("pe_O"), sem("da_done"), sem("dv_done")
        block = ctx.enter_context(nc.Block())

        def quads(eng, body):
            with eng.Fori(0, NT // 2) as pair:
                for u in range(2):
                    for im in range(NB):
                        for k in range(NQD):
                            body(pair, pair * NB + (u * NB + im) // 2, pair * (2 * NB * NQD) + ((u * NB + im) * NQD + k), u, im, k)

        @block.sync
        def _(sp):
            for i in range(2):
                sp.sem_inc(y_out[i], 16)
            hv = hs.rearrange("c h r (q n) -> c h r q n", q=B // NB)
            yv = y.rearrange("b h (k r) c -> b r h k c", r=NWB)

            def load_h(q, r, part):
                c0, c1 = part * (C // NB), (part + 1) * (C // NB)
                src = hv[c0:c1, HB * OH - H:, r, bass.ds(q, 1), :].rearrange("c h q n -> h c (q n)")
                sp.dma_start(ht[r % 2][:, c0:c1, :], src).then_inc(h_in[r % 2], 16)

            def load_x(q, r, im):
                src = x1[:, EDGE:EDGE + H, bass.ds(q * NB + im, 1), r, :, :].rearrange("g h a c w -> h g (a c w)")
                sp.dma_start(xt[im % 2][:, :, :].rearrange("p (g c) w -> p g (c w)", g=G), src).then_inc(x_in[im % 2], 16)

            def round_(q, last):
                for r in range(NWB):
                    for im in range(NB):
                        if r + 1 < NWB:
                            load_h(q, r + 1, im)
                        elif not last:
                            load_h(q + 1, 0, im)
                        sp.wait_ge(v_done, q * (NWB * NB * NQD) + ((r * NB + im + 1) * NQD + 2))
                        sp.dma_start(yv[bass.ds(q * NB + im, 1), r].rearrange("a h k c -> (a h) k c"),
                                     yt[im % 2][:, :, :]).then_inc(y_out[im % 2], 16)
                        dr, im2 = divmod(im + 2, NB)
                        if r + dr < NWB:
                            load_x(q, r + dr, im2)
                        elif not last:
                            load_x(q + 1, 0, im2)

            for part in range(NB):
                load_h(0, 0, part)
            for i in range(2):
                load_x(0, 0, i)
            with sp.Fori(0, B // NB - 1) as q:
                round_(q, False)
            round_(B // NB - 1, True)
            for i in range(2):
                sp.wait_ge(y_out[i], 16 * (TILES // 2 + 1))

        @block.tensor
        def _(pe):
            pe.sem_inc(pe_O, 2)

            def body(pair, ipair, n, u, im, k):
                r = k % 2
                if im == 0 and k == 0:
                    pe.wait_ge(h_in[u], (pair + 1) * (16 * NB))
                pe.wait_ge(a_done, n + 1)
                for w in range(4):
                    last = pe.transpose(pT[r][:, w * P:(w + 1) * P], ht[u][:, :, im * WB + 4 * k + w], s["ident"][:, :])
                last.then_inc(pe_T, 1)
                pe.wait_ge(v_done, n + 1)
                pe.matmul(pO[r][:, :], s["ones3"][0:3, :], s["b_o"][0:3, :, :], start=True, stop=False)
                pe.wait_ge(a_done, n + 3)
                for w in range(4):
                    last = pe.matmul(pO[r][:, w * C:(w + 1) * C], hT[r][:, w, :], s["wout"][:, :], start=False, stop=w == 3)
                last.then_inc(pe_O, 1)

            quads(pe, body)

        @block.scalar
        def _(act):
            act.sem_inc(a_done, 2)

            def body(pair, ipair, n, u, im, k):
                r = k % 2
                act.wait_ge(pe_T, n + 1)
                act.wait_ge(pe_O, n + 1)
                act.activation(view(hT[r][:, 0, P - 1:P], [P, 4], [-1, P]),
                               pT[r][:, :].rearrange("p (w h) -> p w h", h=P), ACT.Copy).then_inc(a_done, 1)

            quads(act, body)

        @block.vector
        def _(v):
            v.sem_inc(v_done, 2)

            def body(pair, ipair, n, u, im, k):
                r, i = k % 2, im % 2
                if k == 0:
                    v.wait_ge(x_in[i], (ipair + 1) * 16)
                    v.wait_ge(y_out[i], (ipair + 1) * 16)
                v.wait_ge(pe_O, n + 3)
                v.tensor_tensor(yt[i][:, 4 * k:4 * k + 4, :], view(xt[i][:, 0, 4 * k:4 * k + 1], [1, 4], [WB, C]),
                                pO[r][:, :].rearrange("p (w c) -> p w c", c=C), ALU.add).then_inc(v_done, 1)

            quads(v, body)


def build(nc, d, y):
    with ExitStack() as ctx:
        def sb(name, shape, dt=F32):
            return ctx.enter_context(nc.sbuf_tensor(name, shape, dt))

        s = {
            "ident": sb("ident", [P, P]), "count": sb("count", [P, 2, P]), "ones3": sb("ones3", [3, P], BF16),
            "tiny": sb("tiny", [P, 1]), "scale_o": sb("scale_o", [P, 1]), "bias_o": sb("bias_o", [P, 1]),
            "wout": sb("wout", [C, C]), "b_o": sb("b_o", [3, 4, C], BF16), "apad": sb("apad", [P, C, 2, 2]),
        }
        rows_dram = nc.dram_tensor("rows_dram", (C, 3 * (NQ + NWB - 1) * RW), F32).ap()
        x1 = nc.dram_tensor("x1", (G, HPAD, B, NWB, CG, WB), F32).ap()
        hs = nc.dram_tensor("hs", (C, HB * OH, NWB, B * WB), F32).ap()
        with ExitStack() as ctx0:
            def sb0(name, shape, dt=F32):
                return ctx0.enter_context(nc.sbuf_tensor(name, shape, dt))

            s.update({
                "nident": sb0("nident", [P, P]), "half": sb0("half", [P, 1]), "mask": sb0("mask", [C, G]),
                "ones_n": sb0("ones_n", [P, P]), "wfi": sb0("wfi", [C, 2 * C]), "wd": sb0("wd", [C, C]),
                "km": sb0("km", [2 * TAPS * TAPS, 4 * CH]), "b_fi": sb0("b_fi", [3, 2, 2 * C], BF16),
                "b_d": sb0("b_d", [3, 4, C], BF16), "rstd": sb0("rstd", [C, B]), "nmr": sb0("nmr", [C, B]),
            })
            setup(nc, d, s, rows_dram)
            stats_of_x(nc, d["x"], s["rstd"], s["nmr"], s["ones_n"], s["mask"])
            layer0(nc, d["x"], x1, d["basis"], s)
        layer1_conv(nc, x1, hs, rows_dram, s)
        layer1_out(nc, x1, hs, y, s)


def constants():
    i = np.arange(TAPS) + (H - TAPS) // 2
    kw, kh = np.arange(W), np.arange(H)
    ang = 2 * np.pi * ((kh[None, None, None, :] * i[:, None, None, None]
                        + kw[None, None, :, None] * i[None, :, None, None]) % H) / H
    ang = ang.reshape(TAPS * TAPS, WB, NWB, H).transpose(0, 2, 1, 3).reshape(TAPS * TAPS, W, H)
    basis = np.concatenate([np.cos(ang), np.sin(ang)]).astype(np.float32)
    sign = np.ones((2 * TAPS * TAPS, 4 * CH), np.float32)
    sign[TAPS * TAPS:, CH:2 * CH] = -1
    sign[TAPS * TAPS:, 3 * CH:] = -1
    mask = (np.arange(C)[:, None] // CG == np.arange(G)[None]).astype(np.float32)
    count = np.zeros((NWB, IH, 2, P), np.float32)
    count[:, EDGE:EDGE + OH, 0] = (HB - 1) * WB * CG / 2 / (H * W * CG)
    count[:, EDGE:EDGE + H - (HB - 1) * OH, 1] = WB * CG / 2 / (H * W * CG)
    return {"count": count.reshape(P, 2, P), "basis": basis, "km_sign": sign, "ident": np.eye(P, dtype=np.float32), "mask": mask}


def kernel(**inputs):
    import concourse.bacc as bacc
    from concourse.bass_utils import run_bass_kernel_spmd

    a = {k: np.asarray(v) for k, v in inputs.items()}

    def taps_first(k):
        return np.transpose(k.reshape(k.shape[0], -1))

    ar, ai, br, bi = (taps_first(a[f"L0_conv_{n}"]) for n in ("A_real", "A_imag", "B_real", "B_imag"))
    km = np.concatenate([np.concatenate([ar, ai, br, bi], 1), np.concatenate([ai, ar, bi, br], 1)], 0)
    taps = np.stack([np.transpose(a[f"L1_conv_{n}"], (0, 2, 1))[:, :, ::-1] for n in ("gate_B_kernel", "B_kernel", "gate_A_kernel")], 1)
    apad = np.zeros((NWB, OH, C, 2, 2), np.float32)
    for i in range(TAPS):
        hb, row = divmod((i - EDGE) % H, OH)
        for j in range(TAPS):
            k, r = divmod((j - EDGE) % W, NWB)
            apad[r, OH - 1 - row, :, int(hb > 0), int(k > 0)] = a["L1_conv_A_kernel"][:, i, j]
    arrays = {
        "x": a["x"], "Wf": a["L0_conv_Wf"], "Wi": a["L0_conv_Wi"], "Wd": a["L0_conv_Wd"], "W_out": a["L1_conv_W_out"],
        "bf": a["L0_conv_bf"][None], "bi": a["L0_conv_bi"][None], "bd": a["L0_conv_bd"][None], "b_out": a["L1_conv_b_out"][None],
        "km": km, "taps": taps, "apad": apad.reshape(NWB * OH, C, 2, 2), **constants(),
    }
    arrays = {f"in_{k}": np.ascontiguousarray(v) for k, v in arrays.items()}
    nc = bacc.Bacc("TRN2", target_bir_lowering=False, num_devices=1)
    d = {k[3:]: nc.dram_tensor(k, v.shape, mybir.dt.from_np(v.dtype), kind="ExternalInput").ap() for k, v in arrays.items()}
    y = nc.dram_tensor("out_y", (B, H, W, C), F32, kind="ExternalOutput").ap()
    build(nc, d, y)
    r = run_bass_kernel_spmd(nc, [arrays], core_ids=[0])
    return r.results[0]["out_y"]
```
